# Optimizing a Trainium2 kernel written in Bass

```python
import numpy as np
import jax
import jax.numpy as jnp

def _softmax(x, axis=-1):
    return jax.nn.softmax(x, axis=axis)

def _gelu(x):
    return jax.nn.gelu(x, approximate=True)

def _silu(x):
    return jax.nn.silu(x)

def _sigmoid(x):
    return jax.nn.sigmoid(x)

def _layernorm(x, axis=-1, eps=1e-05):
    m = jnp.mean(x, axis=axis, keepdims=True)
    v = jnp.var(x, axis=axis, keepdims=True)
    return (x - m) / jnp.sqrt(v + eps)

def _scatter_add(tgt, idx, src, axis=0):
    return tgt.at[idx].add(src)

def _segment_sum(src, seg, n):
    return jax.ops.segment_sum(src, seg, n)
kernel_name = 'mk_perceiver_d1_seqx_r8_52d259'

def setup_inputs(seed: int=0):
    np.random.seed(seed)
    _w = jnp.asarray

    def _rec_inputs():
        import jax
        import jax.numpy as jnp
        _rk = jax.random.key(seed)
        x = -0.000125 + 0.9999 * jax.random.normal(jax.random.fold_in(_rk, 1), (16, 32, 128), jnp.float32)
        _lenS = 32 - jax.random.randint(jax.random.fold_in(_rk, 7), (16,), 0, max(1, 32 // 4) + 1, jnp.int32)
        _lenS2 = 512 - jax.random.randint(jax.random.fold_in(_rk, 8), (16,), 0, max(1, 512 // 4) + 1, jnp.int32)
        _ctx_1024P = jax.random.normal(jax.random.fold_in(_rk, 11), (16, 16, 128), jnp.float32)
        _ctx_1024c = jax.random.dirichlet(jax.random.fold_in(_rk, 511), 0.3 * jnp.ones((16,), jnp.float32), (16, 512))
        _ctx_1024t = jnp.einsum('bsk,bkd->bsd', _ctx_1024c, _ctx_1024P)
        _ctx_1024t = _ctx_1024t * jax.lax.rsqrt(jnp.mean(jnp.square(_ctx_1024t)) + 1e-12) * 0.953939
        ctx_1024 = -0.000514642 + 1.00011 * (_ctx_1024t + 0.3 * jax.random.normal(jax.random.fold_in(_rk, 611), (16, 512, 128), jnp.float32))
        _validS = jnp.arange(32)[None, :] < _lenS[:, None]
        _validS2 = jnp.arange(512)[None, :] < _lenS2[:, None]
        _causal = jnp.tril(jnp.ones((32, 32), dtype=bool))
        mask_BxS2_bf1 = jnp.ones((16, 512), dtype=bool)
        return (x, ctx_1024, mask_BxS2_bf1)
    x, ctx_1024, mask_BxS2_bf1 = _rec_inputs()

    def _L0_xattn_setup():
        import jax, jax.numpy as jnp
        import numpy as np
        EPS = 1e-06
        NUM_HEADS = 16
        DIM_HEADS = 64

        def _ln(x, scale, bias):
            mu = jnp.mean(x, axis=-1, keepdims=True)
            var = jnp.mean(jnp.square(x - mu), axis=-1, keepdims=True)
            return (x - mu) * jax.lax.rsqrt(var + EPS) * scale + bias
        key = jax.random.key(seed)
        ks = jax.random.split(key, 8)
        b, n, m, dim, ctx_dim = (8, 512, 32, 128, 128)
        inner = NUM_HEADS * DIM_HEADS
        x = jax.random.normal(ks[0], (b, n, dim), dtype=jnp.float32)
        context = jax.random.normal(ks[1], (b, m, ctx_dim), dtype=jnp.float32)
        mask = jnp.ones((b, m), dtype=bool)
        Wq = jax.random.normal(ks[2], (dim, inner), dtype=jnp.float32) / np.sqrt(dim)
        Wkv = jax.random.normal(ks[3], (ctx_dim, 2 * inner), dtype=jnp.float32) / np.sqrt(ctx_dim)
        null_kv = jax.random.normal(ks[4], (2, DIM_HEADS), dtype=jnp.float32)
        Wo = jax.random.normal(ks[5], (inner, dim), dtype=jnp.float32) / np.sqrt(inner)
        return {'x': x, 'context': context, 'mask': mask, 'ln1_s': jnp.ones((dim,), jnp.float32), 'ln1_b': jnp.zeros((dim,), jnp.float32), 'lnc_s': jnp.ones((ctx_dim,), jnp.float32), 'lnc_b': jnp.zeros((ctx_dim,), jnp.float32), 'Wq': Wq, 'Wkv': Wkv, 'null_kv': null_kv, 'Wo': Wo, 'lno_s': jnp.ones((dim,), jnp.float32), 'lno_b': jnp.zeros((dim,), jnp.float32)}
    _L0_xattn_all = _L0_xattn_setup()
    _L0_xattn_in = {k: v for k, v in _L0_xattn_all.items() if k in ('ln1_s', 'ln1_b', 'lnc_s', 'lnc_b', 'Wq', 'Wkv', 'null_kv', 'Wo', 'lno_s', 'lno_b')}
    del _L0_xattn_all

    def _L0_attn_setup():
        import jax, jax.numpy as jnp
        import numpy as np
        B, L, C, H, W = (4, 512, 128, 16, 64)
        D = C // H
        STRIDE = W // 2

        def _local_attention(x, w_qkv, b_qkv, w_out, b_out):
            b, l, c = x.shape
            pad = -l % W
            x = jnp.pad(x, ((0, 0), (0, pad), (0, 0)))
            lp = l + pad
            qkv = (x @ w_qkv + b_qkv).reshape(b, lp, 3, H, D).transpose(2, 0, 3, 1, 4)
            q, k, v = (qkv[0], qkv[1], qkv[2])
            nw = (lp - W) // STRIDE + 1
            idx = jnp.arange(nw)[:, None] * STRIDE + jnp.arange(W)[None, :]
            qw = q[:, :, idx, :]
            kw = k[:, :, idx, :]
            vw = v[:, :, idx, :]
            scores = jnp.einsum('bhnqd,bhnkd->bhnqk', qw, kw) / jnp.sqrt(jnp.float32(D))
            probs = jax.nn.softmax(scores, axis=-1)
            ow = jnp.einsum('bhnqk,bhnkd->bhnqd', probs, vw)
            o = ow.transpose(0, 2, 3, 1, 4).reshape(b, nw * W, c)
            o = o @ w_out + b_out
            return o[:, :l, :]
        key = jax.random.key(seed)
        k0, k1, k2 = jax.random.split(key, 3)
        s = 0.02
        return {'x': jax.random.normal(k0, (B, L, C), jnp.float32), 'w_qkv': jax.random.normal(k1, (C, 3 * C), jnp.float32) * s, 'b_qkv': jnp.zeros((3 * C,), jnp.float32), 'w_out': jax.random.normal(k2, (C, C), jnp.float32) * s, 'b_out': jnp.zeros((C,), jnp.float32)}
    _L0_attn_all = _L0_attn_setup()
    _L0_attn_in = {k: v for k, v in _L0_attn_all.items() if k in ('w_qkv', 'b_qkv', 'w_out', 'b_out')}
    del _L0_attn_all

    def _L0_ffn_setup():
        import jax, jax.numpy as jnp
        import numpy as np
        ALPHA = 1.702
        LIMIT = 9.0
        TOP_K = 2

        def swiglu(x):
            g, v = (x[..., 0::2], x[..., 1::2])
            g = jnp.clip(g, None, LIMIT)
            v = jnp.clip(v, -LIMIT, LIMIT)
            return g * jax.nn.sigmoid(ALPHA * g) * (v + 1)
        key = jax.random.key(seed)
        ks = jax.random.split(key, 6)
        B, L, D = (2, 256, 128)
        E, F = (8, 256)
        s_gate = 1.0 / np.sqrt(D)
        s1 = 1.0 / np.sqrt(D)
        s2 = 1.0 / np.sqrt(F)
        return {'x': jax.random.normal(ks[0], (B, L, D), dtype=jnp.float32), 'gate_w': jax.random.normal(ks[1], (D, E), dtype=jnp.float32) * s_gate, 'dense_1_w': jax.random.normal(ks[2], (E, 2 * F, D), dtype=jnp.float32) * s1, 'dense_1_b': jnp.zeros((E, 2 * F), dtype=jnp.float32), 'dense_2_w': jax.random.normal(ks[3], (E, D, F), dtype=jnp.float32) * s2, 'dense_2_b': jnp.zeros((E, D), dtype=jnp.float32)}
    _L0_ffn_all = _L0_ffn_setup()
    _L0_ffn_in = {k: v for k, v in _L0_ffn_all.items() if k in ('gate_w', 'dense_1_w', 'dense_1_b', 'dense_2_w', 'dense_2_b')}
    del _L0_ffn_all
    return {'x': x, 'ctx_1024': ctx_1024, 'mask_BxS2_bf1': mask_BxS2_bf1, 'L0_xattn_ln1_s': _L0_xattn_in['ln1_s'], 'L0_xattn_ln1_b': _L0_xattn_in['ln1_b'], 'L0_xattn_lnc_s': _L0_xattn_in['lnc_s'], 'L0_xattn_lnc_b': _L0_xattn_in['lnc_b'], 'L0_xattn_Wq': _L0_xattn_in['Wq'], 'L0_xattn_Wkv': _L0_xattn_in['Wkv'], 'L0_xattn_null_kv': _L0_xattn_in['null_kv'], 'L0_xattn_Wo': _L0_xattn_in['Wo'], 'L0_xattn_lno_s': _L0_xattn_in['lno_s'], 'L0_xattn_lno_b': _L0_xattn_in['lno_b'], 'L0_attn_w_qkv': _L0_attn_in['w_qkv'], 'L0_attn_b_qkv': _L0_attn_in['b_qkv'], 'L0_attn_w_out': _L0_attn_in['w_out'], 'L0_attn_b_out': _L0_attn_in['b_out'], 'L0_ffn_gate_w': _L0_ffn_in['gate_w'], 'L0_ffn_dense_1_w': _L0_ffn_in['dense_1_w'], 'L0_ffn_dense_1_b': _L0_ffn_in['dense_1_b'], 'L0_ffn_dense_2_w': _L0_ffn_in['dense_2_w'], 'L0_ffn_dense_2_b': _L0_ffn_in['dense_2_b']}

def reference(x, ctx_1024, mask_BxS2_bf1, L0_xattn_ln1_s, L0_xattn_ln1_b, L0_xattn_lnc_s, L0_xattn_lnc_b, L0_xattn_Wq, L0_xattn_Wkv, L0_xattn_null_kv, L0_xattn_Wo, L0_xattn_lno_s, L0_xattn_lno_b, L0_attn_w_qkv, L0_attn_b_qkv, L0_attn_w_out, L0_attn_b_out, L0_ffn_gate_w, L0_ffn_dense_1_w, L0_ffn_dense_1_b, L0_ffn_dense_2_w, L0_ffn_dense_2_b):
    import jax
    import jax.numpy as jnp

    def _L0_xattn_ref(x, context, mask, ln1_s, ln1_b, lnc_s, lnc_b, Wq, Wkv, null_kv, Wo, lno_s, lno_b):
        import jax, jax.numpy as jnp
        import numpy as np
        EPS = 1e-06
        NUM_HEADS = 16
        DIM_HEADS = 64

        def _ln(x, scale, bias):
            mu = jnp.mean(x, axis=-1, keepdims=True)
            var = jnp.mean(jnp.square(x - mu), axis=-1, keepdims=True)
            return (x - mu) * jax.lax.rsqrt(var + EPS) * scale + bias
        b, n, _ = x.shape
        h, d = (NUM_HEADS, DIM_HEADS)
        scale = h ** (-0.5)
        xn = _ln(x, ln1_s, ln1_b)
        cn = _ln(context, lnc_s, lnc_b)
        q = xn @ Wq
        kv = cn @ Wkv
        k, v = jnp.split(kv, 2, axis=-1)

        def to_heads(t):
            return t.reshape(t.shape[0], t.shape[1], h, d).transpose(0, 2, 1, 3)
        q, k, v = (to_heads(q), to_heads(k), to_heads(v))
        nk = jnp.broadcast_to(null_kv[0], (b, h, 1, d))
        nv = jnp.broadcast_to(null_kv[1], (b, h, 1, d))
        k = jnp.concatenate((nk, k), axis=2)
        v = jnp.concatenate((nv, v), axis=2)
        sim = jnp.einsum('bhid,bhjd->bhij', q * scale, k)
        mfull = jnp.pad(mask, ((0, 0), (1, 0)), constant_values=True)[:, None, None, :]
        max_neg = -jnp.finfo(sim.dtype).max
        sim = jnp.where(mfull, sim, max_neg)
        attn = jax.nn.softmax(sim, axis=-1)
        out = jnp.einsum('bhij,bhjd->bhid', attn, v)
        out = out.transpose(0, 2, 1, 3).reshape(b, n, h * d)
        out = out @ Wo
        return _ln(out, lno_s, lno_b)

    def _L0_attn_ref(x, w_qkv, b_qkv, w_out, b_out):
        import jax, jax.numpy as jnp
        import numpy as np
        B, L, C, H, W = (4, 512, 128, 16, 64)
        D = C // H
        STRIDE = W // 2

        def _local_attention(x, w_qkv, b_qkv, w_out, b_out):
            b, l, c = x.shape
            pad = -l % W
            x = jnp.pad(x, ((0, 0), (0, pad), (0, 0)))
            lp = l + pad
            qkv = (x @ w_qkv + b_qkv).reshape(b, lp, 3, H, D).transpose(2, 0, 3, 1, 4)
            q, k, v = (qkv[0], qkv[1], qkv[2])
            nw = (lp - W) // STRIDE + 1
            idx = jnp.arange(nw)[:, None] * STRIDE + jnp.arange(W)[None, :]
            qw = q[:, :, idx, :]
            kw = k[:, :, idx, :]
            vw = v[:, :, idx, :]
            scores = jnp.einsum('bhnqd,bhnkd->bhnqk', qw, kw) / jnp.sqrt(jnp.float32(D))
            probs = jax.nn.softmax(scores, axis=-1)
            ow = jnp.einsum('bhnqk,bhnkd->bhnqd', probs, vw)
            o = ow.transpose(0, 2, 3, 1, 4).reshape(b, nw * W, c)
            o = o @ w_out + b_out
            return o[:, :l, :]
        return _local_attention(x, w_qkv, b_qkv, w_out, b_out)

    def _L0_ffn_ref(x, gate_w, dense_1_w, dense_1_b, dense_2_w, dense_2_b):
        import jax, jax.numpy as jnp
        import numpy as np
        ALPHA = 1.702
        LIMIT = 9.0
        TOP_K = 2

        def swiglu(x):
            g, v = (x[..., 0::2], x[..., 1::2])
            g = jnp.clip(g, None, LIMIT)
            v = jnp.clip(v, -LIMIT, LIMIT)
            return g * jax.nn.sigmoid(ALPHA * g) * (v + 1)
        B, L, D = x.shape
        xf = x.reshape(B * L, D)
        gate = xf @ gate_w
        weights, sel = jax.lax.top_k(gate, k=TOP_K)
        weights = jax.nn.softmax(weights, axis=-1)
        h = jnp.einsum('ecd,td->tec', dense_1_w, xf) + dense_1_b[None]
        h = swiglu(h)
        y = jnp.einsum('edf,tef->ted', dense_2_w, h) + dense_2_b[None]
        y_sel = jnp.take_along_axis(y, sel[:, :, None], axis=1)
        out = jnp.einsum('tkd,tk->td', y_sel, weights)
        return out.reshape(B, L, D)
    x = x + _L0_xattn_ref(_layernorm(x, axis=-1), ctx_1024, mask_BxS2_bf1, L0_xattn_ln1_s, L0_xattn_ln1_b, L0_xattn_lnc_s, L0_xattn_lnc_b, L0_xattn_Wq, L0_xattn_Wkv, L0_xattn_null_kv, L0_xattn_Wo, L0_xattn_lno_s, L0_xattn_lno_b)
    x = x + _L0_attn_ref(_layernorm(x, axis=-1), L0_attn_w_qkv, L0_attn_b_qkv, L0_attn_w_out, L0_attn_b_out)
    x = x + _L0_ffn_ref(_layernorm(x, axis=-1), L0_ffn_gate_w, L0_ffn_dense_1_w, L0_ffn_dense_1_b, L0_ffn_dense_2_w, L0_ffn_dense_2_b)
    return x

_drawn_inputs = setup_inputs


def setup_inputs(seed=0):
    import zlib

    import numpy as np

    out = dict(_drawn_inputs(seed))
    spreads = {'L0_xattn_ln1_s': (1.0, 0.2),
     'L0_xattn_ln1_b': (0.0, 0.1),
     'L0_xattn_lnc_s': (1.0, 0.2),
     'L0_xattn_lnc_b': (0.0, 0.1),
     'L0_xattn_lno_s': (1.0, 0.2),
     'L0_xattn_lno_b': (0.0, 0.1),
     'L0_attn_b_qkv': (0.0, 0.1),
     'L0_attn_b_out': (0.0, 0.1),
     'L0_ffn_dense_1_b': (0.0, 0.1),
     'L0_ffn_dense_2_b': (0.0, 0.1)}
    factors = {}
    for name, (base, spread) in spreads.items():
        noise = np.random.default_rng([zlib.crc32(name.encode()), seed]).standard_normal(out[name].shape)
        drawn = base * np.exp(spread * noise) if base else spread * noise
        out[name] = jnp.asarray(drawn.astype(out[name].dtype))
    for name, factor in factors.items():
        out[name] = (out[name] * factor).astype(out[name].dtype)
    return out
```

```python
from contextlib import ExitStack

import concourse.bass as bass
from concourse import mybir

ALU = mybir.AluOpType
ACT = mybir.ActivationFunctionType
AX = mybir.AxisListType
F32 = mybir.dt.float32
I32 = mybir.dt.int32
BF16 = mybir.dt.bfloat16
U8 = mybir.dt.uint8

P = 128
B, N, C = 16, 32, 128
M = 512
H, D = 16, 64
GB = P // N
G = B // GB
T = M // P
HG = H // GB
KC = H * D // P
LD = C // 16
LR = 32 // LD
LJ = N + 1
PADS = 64 - N
E = 8
L_STEPS = 39
SCALE = H ** -0.5
BIG = 3e38
MAGIC = 0x5F3759DF

V_LN1S, V_LN1B, V_LNCS, V_LNCB, V_BQ, V_BK, V_BV, V_NK, V_NV = range(9)
V_B1 = 9
V_N = V_B1 + E * 4
K_ID, K_R, K_V, K_N = 0, P, P + LR, 2 * P + LR
K_IOTA = K_N
K_COLS = K_N + E


def at(t, i):
    return t[i] if isinstance(i, int) else t[bass.ds(i, 1)].squeeze(0)


def col(t, i):
    return t[:, i] if isinstance(i, int) else t[:, bass.ds(i, 1)].squeeze(1)


class Chain:

    def __init__(self, eng, sem):
        self.eng, self.sem, self.n, self.base = eng, sem, 0, 0

    def link(self, ins):
        ins.then_inc(self.sem, 1)
        self.n += 1
        self.eng.wait_ge(self.sem, self.base + self.n)

    def loop(self, it, per_body):
        self.start = self.n
        self.base = it * per_body
        self.per_body = per_body

    def end(self, times):
        assert self.n - self.start == self.per_body, (self.n - self.start, self.per_body)
        self.n += (times - 1) * self.per_body
        self.base = 0


def perceiver(nc, x, ctx_in, mask, vec, rows, const, wqT, wkT, wvT, wv, wo, wqkv, wout, gate, w1, w2, b2, out):
    with ExitStack() as ctx:
        def sb(name, shape, dt=F32):
            return ctx.enter_context(nc.sbuf_tensor(name, shape, dt))

        def ps(name, shape=(P, 512)):
            return ctx.enter_context(nc.psum_tensor(name, list(shape), F32))

        def sem(name):
            return ctx.enter_context(nc.semaphore(name))

        X = sb("X", [P, G, C])
        VEC = sb("VEC", [P, V_N])
        ROWS = sb("ROWS", [P, 3, C])
        CON = sb("CON", [P, K_COLS])
        WqT = sb("WqT", [P, KC, C])
        WkT = sb("WkT", [P, KC, C])
        WvT = sb("WvT", [P, KC, C])
        Wv = sb("Wv", [P, H * D])
        Wo = sb("Wo", [P, KC, C])
        Wqkv = sb("Wqkv", [P, 3 * C])
        Wout = sb("Wout", [P, C])
        Gate = sb("Gate", [P, E])
        B2 = sb("B2", [E, C])
        CTX = sb("CTX", [P, B, T, C])
        MK8 = sb("MK8", [P, B, M], U8)
        MB = sb("MB", [P, 2, M], BF16)
        A = sb("A", [P, H, C])
        Bm = sb("Bm", [P, H, C])
        U = sb("U", [P, P])
        NVW = sb("NVW", [P, C])
        NKblk = sb("NKblk", [P, KC * P])
        NVblk = sb("NVblk", [P, KC * P])
        nvk = sb("nvk", [P, KC])
        xnT = sb("xnT", [P, G * P])
        sn_pad = sb("sn_pad", [P, G * P])
        SNR = sb("SNR", [P, B, N])
        rowtmp = sb("rowtmp", [P, G, C])

        NC = sb("NC", [P, GB, T, C])
        cnT = sb("cnT", [P, 2, M])
        QK = sb("QK", [P, GB, H, N])
        SM = sb("SM", [P, 2, HG, M])
        PT = sb("PT", [P, T, M])
        AC = sb("AC", [P, H, P])
        PNR = sb("PNR", [P, GB, N])
        PNT = sb("PNT", [P, P])
        OUT1 = sb("OUT1", [P, G, C])
        cstat = sb("cstat", [P, GB * T, 6])
        cmv = sb("cmv", [P, GB * T, 2])
        crs = sb("crs", [P, GB * T])
        mrow = sb("mrow", [P, 2, HG])
        mx4 = sb("mx4", [P, HG])
        negm = sb("negm", [P, 2, HG])
        snm = sb("snm", [P, 2, HG])
        rsum = sb("rsum", [P, 2, HG])
        pn = sb("pn", [P, 2, HG])
        lsum = sb("lsum", [P, HG])
        rinv = sb("rinv", [P, 2, HG])
        xstat = sb("xstat", [P, G, 6])
        xmv = sb("xmv", [P, G, 2])
        xrs = sb("xrs", [P, G])
        nt_v = sb("nt_v", [P, GB * T])
        nt_i = sb("nt_i", [P, GB * T], I32)
        nt_a = sb("nt_a", [P, GB * T])

        y1 = sb("y1", [P, C])
        xg = sb("xg", [P, C])
        xgT = sb("xgT", [P, P])
        XR = sb("XR", [P, GB, LR, N])
        qT = sb("qT", [P, P])
        kTe = sb("kTe", [P, GB, LJ])
        Kbd = sb("Kbd", [P, GB, LR, LJ])
        Vbd = sb("Vbd", [P, GB, C])
        SL = sb("SL", [P, 16, LJ])
        PL = sb("PL", [P, 16, N])
        PLT = sb("PLT", [P, 4, P])
        lmax = sb("lmax", [P, 16])
        lden = sb("lden", [P, 16])
        lrec = sb("lrec", [P, 16])
        oT = sb("oT", [P, P])

        fn = sb("fn", [P, G, C])
        fnT = sb("fnT", [P, G * P])
        gt = sb("gt", [P, G, E])
        g_is1 = sb("g_is1", [P, G, E])
        g_a = sb("g_a", [P, G, E])
        g_rest = sb("g_rest", [P, G, E])
        g_is2 = sb("g_is2", [P, G, E])
        gw = sb("gw", [P, G, E])
        gm1 = sb("gm1", [P, G])
        gm2 = sb("gm2", [P, G])
        gi = sb("gi", [P, G])
        gd = sb("gd", [P, G])
        gp1 = sb("gp1", [P, G])
        gp2 = sb("gp2", [P, G])
        gwT = sb("gwT", [E, G * P])
        b1v = sb("b1v", [P, E, 2])
        W1s = [sb(f"W1s{i}", [P, 2, 2, P]) for i in range(2)]
        W2s = [sb(f"W2s{i}", [P, 2, C]) for i in range(2)]
        hg, hv, hs, hT = SM[:, 0, 0:2, :], SM[:, 0, 2:4, :], SM[:, 1, 0:2, :], SM[:, 1, 2:4, :]

        pS = [ps("pS0"), ps("pS1")]
        pP = [ps("pP0"), ps("pP1")]
        pA, pC = ps("pA"), ps("pC")
        pM = [ps("pM0"), ps("pM1")]

        ld_x, ld_vec, ld_con, ld_rows = sem("ld_x"), sem("ld_vec"), sem("ld_con"), sem("ld_rows")
        ld_wq, ld_wk, ld_wvT, ld_wv, ld_wo = sem("ld_wq"), sem("ld_wk"), sem("ld_wvT"), sem("ld_wv"), sem("ld_wo")
        ld_ctx = [sem(f"ld_ctx{g}") for g in range(G)]
        ld_mask = sem("ld_mask")
        ld_loc, ld_wl = sem("ld_loc"), sem("ld_wl")
        ld_e = [sem("ld_e0"), sem("ld_e1")]
        dve_step, act_step, pool_step, pe_step = sem("dve_step"), sem("act_step"), sem("pool_step"), sem("pe_step")
        mask_copied = sem("mask_copied")
        mask_ready = sem("mask_ready")
        wait_passed = {e.engine: sem(f"wait_passed_{n}") for n, e in
                       (("dve", nc.vector), ("pe", nc.tensor), ("pool", nc.gpsimd))}
        blk_zero = sem("blk_zero")
        x_normed, xT_ready, xT_copied = sem("x_normed"), sem("xT_ready"), sem("xT_copied")
        nk_placed, u_ready, u_copied = sem("nk_placed"), sem("u_ready"), sem("u_copied")
        vb_ready, nv_placed, nvw_ready, nvw_copied = sem("vb_ready"), sem("nv_placed"), sem("nvw_ready"), sem("nvw_copied")
        wA_ready, wA_copied = sem("wA_ready"), sem("wA_copied")
        wB_ready, wB_copied = sem("wB_ready"), sem("wB_copied")
        masked = sem("masked")
        sn_ready, sn_copied, sn_rows = sem("sn_ready"), sem("sn_copied"), sem("sn_rows")
        ctx_normed, cT_ready, cT_copied = sem("ctx_normed"), sem("cT_ready"), sem("cT_copied")
        qk_ready, qk_copied = sem("qk_ready"), sem("qk_copied")
        scores_ready, shift_ready, exp_done = sem("scores_ready"), sem("shift_ready"), sem("exp_done")
        recip_ready, probs_normed = sem("recip_ready"), sem("probs_normed")
        probsT_ready, ptA_copied, ptD_copied = sem("probsT_ready"), sem("ptA_copied"), sem("ptD_copied")
        pv_ready, ac_copied, pnT_ready = sem("pv_ready"), sem("ac_copied"), sem("pnT_ready")
        out_ready, out_copied = sem("out_ready"), sem("out_copied")
        l_xn, l_xT, l_xTc = sem("l_xn"), sem("l_xT"), sem("l_xTc")
        l_q, l_k, l_v = sem("l_q"), sem("l_k"), sem("l_v")
        l_qc, l_kc, l_vc = sem("l_qc"), sem("l_kc"), sem("l_vc")
        l_s, l_sub, l_exp, l_p, l_pT, l_pTc = (sem("l_s"), sem("l_sub"), sem("l_exp"), sem("l_p"), sem("l_pT"),
                                               sem("l_pTc"))
        l_o, l_oc, l_y, l_yc = sem("l_o"), sem("l_oc"), sem("l_y"), sem("l_yc")
        f_n, f_T, f_Tc, f_g, f_gd, f_ge, f_w, f_wT, f_wTc, f_b, f_bc = (
            sem(f"f_{n}") for n in ("n", "T", "Tc", "g", "gd", "ge", "w", "wT", "wTc", "b", "bc"))
        e_h, e_hc, e_sg, e_hT, e_y, e_yc = (sem(f"e_{n}") for n in ("h", "hc", "sg", "hT", "y", "yc"))
        x1_ready, x2_ready, st_out = sem("x1_ready"), sem("x2_ready"), sem("st_out")

        def passed(eng, i):
            if not isinstance(i, int):
                eng.sem_inc(wait_passed[eng.engine], 1)

        ident = CON[:, K_ID:K_ID + P]
        block = ctx.enter_context(nc.Block())

        @block.sync
        def _(sp):
            sp.dma_start(X[:, :, :], x.rearrange("(g p) c -> p g c", p=P)).then_inc(ld_x, 16)
            sp.dma_start(VEC[:, :], vec).then_inc(ld_vec, 16)
            sp.dma_start(CON[:, :], const).then_inc(ld_con, 16)
            sp.dma_start(WqT[:, :, :], wqT.rearrange("(k p) c -> p k c", p=P)).then_inc(ld_wq, 16)
            sp.dma_start(WkT[:, :, :], wkT.rearrange("(k p) c -> p k c", p=P)).then_inc(ld_wk, 16)
            for g in range(G):
                sp.dma_start(CTX[:, GB * g:GB * (g + 1), :, :],
                             ctx_in[GB * g * M:GB * (g + 1) * M, :].rearrange("(b p t) c -> p b t c", p=P, t=T)
                             ).then_inc(ld_ctx[g], 16)
                if g == 0:
                    sp.dma_start(Wv[:, :], wv).then_inc(ld_wv, 16)
                    sp.dma_start(WvT[:, :, :], wvT.rearrange("(k p) c -> p k c", p=P)).then_inc(ld_wvT, 16)
                    sp.dma_start(Wo[:, :, :], wo.rearrange("(k p) c -> p k c", p=P)).then_inc(ld_wo, 16)
            sp.dma_start(ROWS[:, :, :], rows.broadcast_to([P, 3, C])).then_inc(ld_rows, 16)
            sp.dma_start(Wqkv[:, :], wqkv).then_inc(ld_loc, 16)
            sp.dma_start(Wout[:, :], wout).then_inc(ld_loc, 16)
            sp.dma_start(Gate[:, :], gate).then_inc(ld_loc, 16)
            sp.dma_start(B2[:, :], b2).then_inc(ld_loc, 16)
            for i in range(2):
                sp.dma_start(W1s[i][:, :, :, :], w1[i]).then_inc(ld_e[i], 16)
                sp.dma_start(W2s[i][:, :, :], w2[i]).then_inc(ld_e[i], 16)
            with sp.Fori(1, E // 2) as it:
                for i in range(2):
                    sp.wait_ge(e_y, it * 2 - 1 + i)
                    sp.dma_start(W1s[i][:, :, :, :], at(w1, it * 2 + i)).then_inc(ld_e[i], 16)
                    sp.dma_start(W2s[i][:, :, :], at(w2, it * 2 + i)).then_inc(ld_e[i], 16)
            sp.wait_ge(e_yc, E + 1)
            sp.dma_start(out.rearrange("(g p) c -> p g c", p=P), X[:, :, :]).then_inc(st_out, 16)
            sp.wait_ge(st_out, 16)

        @block.gpsimd
        def _(pool):
            pool.memset(NKblk[:, :], 0.0).then_inc(blk_zero, 1)
            pool.memset(NVblk[:, :], 0.0).then_inc(blk_zero, 1)
            pool.memset(PNR[:, :, :], 0.0).then_inc(blk_zero, 1)

            def mask_bias(b, k):
                pool.tensor_copy(MB[:, k, :], col(MK8, b)).then_inc(mask_copied, 1)
                pool.wait_ge(mask_copied, b + 1)
                passed(pool, b)
                pool.tensor_scalar(MB[:, k, :], MB[:, k, :], BIG, -BIG, ALU.mult, ALU.add).then_inc(mask_ready, 1)

            pool.wait_ge(ld_mask, 16)
            mask_bias(0, 0)
            mask_bias(1, 1)

            def normalise(b, k, last=False):
                pool.wait_ge(recip_ready, b + 1)
                passed(pool, b)
                for q in range(HG):
                    pool.tensor_scalar(SM[:, k, q, :], SM[:, k, q, :], rinv[:, k, q:q + 1], None,
                                       ALU.mult).then_inc(probs_normed, 1)
                if not last:
                    mask_bias(b + 2, k)

            with pool.Fori(0, B // 2 - 1) as it:
                for k in range(2):
                    normalise(it * 2 + k, k)
            for k in range(2):
                normalise(B - 2 + k, k, True)

        @block.scalar
        def _(act):
            act.dma_start(MK8[:, :, :].rearrange("p b m -> p (b m)"), mask.broadcast_to([P, B * M])).then_inc(ld_mask, 16)

            def copy_cT(b, k, first=False):
                act.wait_ge(cT_ready, b + 1)
                if not first:
                    act.wait_ge(scores_ready, b * HG - HG)
                act.activation(cnT[:, k % 2, :], pC[:, :], ACT.Identity, bias=VEC[:, V_LNCB:V_LNCB + 1],
                               scale=VEC[:, V_LNCS:V_LNCS + 1]).then_inc(cT_copied, 1)

            def copy_qk(g, first=False):
                for q in range(HG):
                    act.wait_ge(qk_ready, g * HG + q + 1)
                    if q == 0 and not first:
                        act.wait_ge(scores_ready, g * GB * HG)
                    act.copy(QK[:, :, GB * q:GB * (q + 1), :].rearrange("p k h i -> p h k i"),
                             pM[q % 2][:, :].rearrange("p (h k i) -> p h k i", h=GB, k=GB)).then_inc(qk_copied, 1)

            def exps(b, k):
                act.wait_ge(shift_ready, b + 1)
                act.activation(pn[:, k % 2, :], snm[:, k % 2, :], ACT.Exp).then_inc(exp_done, 1)
                for q in range(HG):
                    act.activation(SM[:, k % 2, q, :], SM[:, k % 2, q, :], ACT.Exp, bias=negm[:, k % 2, q:q + 1],
                                   scale=SCALE, accum_out=rsum[:, k % 2, q:q + 1]).then_inc(exp_done, 1)

            def copy_pT(b, first=False):
                for t in (0, 2):
                    act.wait_ge(probsT_ready, b * T + t + 1)
                    if t == 0 and not first:
                        act.wait_ge(pv_ready, b)
                    act.copy(PT[:, t, :], pP[t % 2][:, :]).then_inc(ptA_copied, 1)

            def copy_heads(W, q, done):
                for e in range(2):
                    ins = act.copy(W[:, 4 * q + e:4 * q + 4:2, :],
                                   (pP, pS)[q % 2][e][:, 0:2 * C].rearrange("p (a c) -> p a c", a=2))
                ins.then_inc(done, 1)

            act.wait_ge(u_ready, 1)
            act.copy(U[:, :], pC[:, 0:P]).then_inc(u_copied, 1)
            for q in range(H // 4):
                act.wait_ge(wA_ready, q + 1)
                copy_heads(A, q, wA_copied)
            act.wait_ge(sn_ready, 1)
            act.copy(sn_pad[:, :], pM[0][:, :]).then_inc(sn_copied, 1)
            copy_qk(0, True)
            for q in range(H // 4):
                act.wait_ge(wB_ready, q + 1)
                copy_heads(Bm, q, wB_copied)
            act.wait_ge(nvw_ready, 1)
            act.copy(NVW[:, :], pC[:, 0:C]).then_inc(nvw_copied, 1)
            act.wait_ge(ld_vec, 16)
            copy_cT(0, 0, True)
            copy_cT(1, 1, True)
            exps(0, 0)

            def body(it, first=False, last=False):
                for k in range(GB):
                    b = it * GB + k
                    if not (last and k >= GB - 2):
                        copy_cT(b + 2, k)
                    if k == GB - 2 and not last:
                        copy_qk(it + 1)
                    copy_pT(b, first and k == 0)
                    if not (last and k == GB - 1):
                        exps(b + 1, k + 1)
                act.wait_ge(out_ready, it + 1)
                act.copy(col(OUT1, it), pC[:, 0:C]).then_inc(out_copied, 1)

            body(0, first=True)
            with act.Fori(1, G - 1) as it:
                body(it)
            body(G - 1, last=True)

            with act.Fori(0, G) as g:
                act.wait_ge(l_xT, g + 1)
                act.copy(xgT[:, :], pC[:, 0:P])
                act.copy(XR[:, :, :, :], pC[:, 0:P].rearrange("p (b i) -> p b i", b=GB).unsqueeze(2)
                         .broadcast_to([P, GB, LR, N])).then_inc(l_xTc, 1)
                act.wait_ge(l_sub, g + 1)
                act.activation(SL[:, :, :], SL[:, :, :], ACT.Exp).then_inc(l_exp, 1)
                act.wait_ge(l_pT, g + 1)
                act.copy(PLT[:, :, :].rearrange("p a b -> p (a b)"), pP[0][:, :]).then_inc(l_pTc, 1)

            act.wait_ge(f_T, 1)
            act.copy(fnT[:, :], pC[:, :]).then_inc(f_Tc, 1)
            act.wait_ge(f_gd, 1)
            act.activation(gp2[:, :], gd[:, :], ACT.Exp).then_inc(f_ge, 1)
            act.wait_ge(f_wT, 1)
            act.copy(gwT[:, :], pP[1][0:E, :]).then_inc(f_wTc, 1)
            with act.Fori(0, E) as e:
                for i in range(2):
                    act.wait_ge(e_hc, e * 2 + i + 1)
                    act.activation(hs[:, i, :], hg[:, i, :], ACT.Gelu_apprx_sigmoid).then_inc(e_sg, 1)

        @block.tensor
        def _(pe):
            def head_products(L, R, q, done):
                for a in range(2):
                    for e in range(2):
                        ins = pe.matmul((pP, pS)[q % 2][e][:, a * C:(a + 1) * C], L[64 * e:64 * e + 64, 2 * q + a, :],
                                        R[64 * e:64 * e + 64, 2 * q + a, :], start=True, stop=True)
                ins.then_inc(done, 1)

            pe.wait_ge(ld_wq, 16)
            pe.wait_ge(nk_placed, 1)
            for c in range(KC):
                ins = pe.matmul(pC[:, 0:P], WqT[:, c, :], NKblk[:, c * P:(c + 1) * P], start=(c == 0), stop=(c == KC - 1))
            ins.then_inc(u_ready, 1)
            pe.wait_ge(ld_wk, 16)
            for q in range(H // 4):
                if q >= 2:
                    pe.wait_ge(wA_copied, q - 1)
                head_products(WqT, WkT, q, wA_ready)
            pe.wait_ge(x_normed, 1)
            pe.wait_ge(ld_con, 16)
            for g in range(G):
                ins = pe.transpose(pM[1][:, g * P:(g + 1) * P], rowtmp[:, g, :], ident)
            ins.then_inc(xT_ready, 1)
            pe.wait_ge(xT_copied, 1)
            pe.wait_ge(u_copied, 1)
            pe.matmul(pM[0][:, :], U[:, :], xnT[:, :], start=True, stop=True).then_inc(sn_ready, 1)

            def qk(g, first=False):
                for q in range(HG):
                    if not (first and q < 2):
                        pe.wait_ge(qk_copied, g * HG + q - 1)
                    for h in range(4):
                        ins = pe.matmul(pM[q % 2][:, h * P:(h + 1) * P], A[:, 4 * q + h, :],
                                        xnT[:, bass.ds(g * P, P)], start=True, stop=True)
                    ins.then_inc(qk_ready, 1)

            def ctx_T(b, k, first=False):
                pe.wait_ge(ctx_normed, b + 1)
                if not first:
                    pe.wait_ge(cT_copied, b)
                for t in range(T):
                    ins = pe.transpose(pC[:, t * P:(t + 1) * P], NC[:, k, t, :], ident)
                ins.then_inc(cT_ready, 1)

            def scores(b, k, g, first=False):
                pe.wait_ge(cT_copied, b + 1)
                if k == 0:
                    pe.wait_ge(qk_copied, g * HG + HG)
                for q in range(HG):
                    if not (first and q < 2):
                        pe.wait_ge(masked, b * HG + q - 1)
                    pe.matmul(pS[q % 2][:, :], QK[:, k, 4 * q:4 * q + 4, :].rearrange("p h i -> p (h i)"),
                              cnT[:, k % 2, :], start=True, stop=True).then_inc(scores_ready, 1)

            def probs_T(b, k, t, first=False):
                if t == 0:
                    pe.wait_ge(probs_normed, b * HG + HG)
                if not (first and t < 2):
                    pe.wait_ge((ptA_copied, ptD_copied)[t % 2], b * 2 + t // 2)
                for q in range(HG):
                    ins = pe.transpose(pP[t % 2][:, q * P:(q + 1) * P], SM[:, k % 2, q, t * P:(t + 1) * P], ident)
                ins.then_inc(probsT_ready, 1)

            def pv(b, k, t, first=False):
                if t == 0 and not first:
                    pe.wait_ge(ac_copied, b)
                pe.wait_ge((ptA_copied, ptD_copied)[t % 2], b * 2 + t // 2 + 1)
                ins = pe.matmul(pA[:, :], NC[:, k, t, :], PT[:, t, :], start=(t == 0), stop=(t == T - 1))
                if t == T - 1:
                    ins.then_inc(pv_ready, 1)

            pe.wait_ge(ld_wv, 16)
            pe.wait_ge(ld_vec, 16)
            for c in range(KC):
                ins = pe.matmul(pA[:, c:c + 1], Wv[:, c * P:(c + 1) * P], VEC[:, V_LNCB:V_LNCB + 1], start=True, stop=True)
            ins.then_inc(vb_ready, 1)
            pe.wait_ge(sn_copied, 1)
            pe.wait_ge(wA_copied, H // 4)
            qk(0, True)
            pe.wait_ge(ld_wvT, 16)
            pe.wait_ge(ld_wo, 16)
            for q in range(H // 4):
                if q >= 2:
                    pe.wait_ge(wB_copied, q - 1)
                head_products(WvT, Wo, q, wB_ready)
            pe.wait_ge(nv_placed, 1)
            for c in range(KC):
                ins = pe.matmul(pC[:, 0:C], NVblk[:, c * P:(c + 1) * P], Wo[:, c, :], start=(c == 0), stop=(c == KC - 1))
            ins.then_inc(nvw_ready, 1)
            pe.wait_ge(nvw_copied, 1)
            pe.wait_ge(wB_copied, H // 4)
            ctx_T(0, 0, True)
            scores(0, 0, 0, True)
            ctx_T(1, 1)

            def body(it, first=False, last=False):
                for k in range(GB):
                    b = it * GB + k
                    if not (last and k == GB - 1):
                        scores(b + 1, (k + 1) % GB, it + (k + 1) // GB)
                    if k == 0 and not first:
                        pe.wait_ge(out_copied, it)
                    if not (last and k >= GB - 2):
                        ctx_T(b + 2, (k + 2) % GB)
                    if k == GB - 2 and not last:
                        qk(it + 1)
                    probs_T(b, k, 0, first and k == 0)
                    probs_T(b, k, 1, first and k == 0)
                    probs_T(b, k, 2)
                    pv(b, k, 0, first and k == 0)
                    probs_T(b, k, 3)
                    for t in range(1, T):
                        pv(b, k, t)
                pe.wait_ge(pnT_ready, it + 1)
                pe.wait_ge(cT_copied, it * GB + GB + (0 if last else 2))
                pe.wait_ge(ac_copied, it * GB + GB)
                for h in range(H):
                    pe.matmul(pC[:, 0:C], AC[:, h, :], Bm[:, h, :], start=(h == 0), stop=False)
                pe.matmul(pC[:, 0:C], PNT[:, :], NVW[:, :], start=False, stop=True).then_inc(out_ready, 1)

            body(0, first=True)
            with pe.Fori(1, G - 1) as it:
                body(it)
            body(G - 1, last=True)

            pe.wait_ge(ld_loc, 64)
            pe.wait_ge(out_copied, G)
            with pe.Fori(0, G) as g:
                pe.wait_ge(l_xn, g + 1)
                pe.transpose(pC[:, 0:P], xg[:, :], ident).then_inc(l_xT, 1)
                pe.wait_ge(l_xTc, g + 1)
                pe.matmul(pM[0][:, 0:P], Wqkv[:, 0:C], xgT[:, :], start=True, stop=True).then_inc(l_q, 1)
                pe.matmul(pM[1][:, 0:P], Wqkv[:, C:2 * C], xgT[:, :], start=True, stop=True).then_inc(l_k, 1)
                for b in range(GB):
                    ins = pe.matmul(pA[:, b * C:(b + 1) * C], XR[:, b, :, :].rearrange("p r i -> p (r i)"),
                                    Wqkv[:, 2 * C:3 * C], start=True, stop=True)
                ins.then_inc(l_v, 1)
                pe.wait_ge(l_qc, g + 1)
                pe.wait_ge(l_kc, g + 1)
                passed(pe, g)
                banks = [pS[0], pS[1], pP[0], pP[1]]
                for b in range(GB):
                    for r in range(4):
                        ins = pe.matmul(banks[r][N * b:N * b + N, 0:LR * LJ], qT[32 * r:32 * r + 32, N * b:N * b + N],
                                        Kbd[32 * r:32 * r + 32, b, :, :].rearrange("p r j -> p (r j)"),
                                        start=True, stop=True)
                ins.then_inc(l_s, 1)
                pe.wait_ge(l_p, g + 1)
                for r in range(4):
                    ins = pe.transpose(pP[0][:, r * P:(r + 1) * P],
                                       PL[:, 4 * r:4 * r + 4, :].rearrange("p h j -> p (h j)"), ident)
                ins.then_inc(l_pT, 1)
                pe.wait_ge(l_pTc, g + 1)
                pe.wait_ge(l_vc, g + 1)
                passed(pe, g)
                for b in range(GB):
                    for r in range(4):
                        ins = pe.matmul(pM[0][32 * r:32 * r + 32, N * b:N * b + N], Vbd[:, b, 32 * r:32 * r + 32],
                                        PLT[:, r, N * b:N * b + N], start=True, stop=True)
                ins.then_inc(l_o, 1)
                pe.wait_ge(l_oc, g + 1)
                pe.matmul(pM[1][:, 0:C], oT[:, :], Wout[:, :], start=True, stop=True).then_inc(l_y, 1)

            pe.wait_ge(f_n, 1)
            for g in range(G):
                ins = pe.transpose(pC[:, g * P:(g + 1) * P], fn[:, g, :], ident)
            ins.then_inc(f_T, 1)
            pe.wait_ge(f_Tc, 1)
            for g in range(G):
                ins = pe.matmul(pP[0][:, g * E:(g + 1) * E], fnT[:, g * P:(g + 1) * P], Gate[:, :], start=True, stop=True)
            ins.then_inc(f_g, 1)
            pe.wait_ge(f_w, 1)
            for g in range(G):
                ins = pe.transpose(pP[1][0:E, g * P:(g + 1) * P], gw[:, g, :], ident)
            ins.then_inc(f_wT, 1)
            pe.wait_ge(f_wTc, 1)
            for g in range(G):
                ins = pe.matmul(pA[:, g * C:(g + 1) * C], gwT[:, g * P:(g + 1) * P], B2[:, :], start=True, stop=True)
            ins.then_inc(f_b, 1)

            def hidden(e, s, loads, first=False):
                pe.wait_ge(ld_e[s], loads)
                for i in range(2):
                    if not first:
                        pe.wait_ge(e_hc, e * 2 + i - 1)
                    for v in range(2):
                        ins = pe.matmul((pS, pP)[i][v][:, :], W1s[s][:, v, i, :], fnT[:, :], start=True, stop=True)
                    ins.then_inc(e_h, 1)

            def down(e, s):
                pe.wait_ge(e_hT, e * 2 + 2)
                pe.wait_ge(e_yc, e + 1)
                for g in range(G):
                    for i in range(2):
                        ins = pe.matmul(pA[:, g * C:(g + 1) * C], hT[:, i, g * P:(g + 1) * P], W2s[s][:, i, :],
                                        start=(i == 0), stop=(i == 1))
                ins.then_inc(e_y, 1)

            hidden(0, 0, 32, True)
            with pe.Fori(0, E // 2 - 1) as it:
                hidden(it * 2 + 1, 1, it * 32 + 32)
                down(it * 2, 0)
                hidden(it * 2 + 2, 0, it * 32 + 64)
                down(it * 2 + 1, 1)
            hidden(E - 1, 1, 16 * E)
            down(E - 2, 0)
            down(E - 1, 1)

        @block.vector
        def _(dve):
            ch = Chain(dve, dve_step)
            link = ch.link

            def b_late(b):
                return not isinstance(b, int) or b >= 2

            def inv_sqrt(out, var, eps, n):
                v, i0, a = nt_v[:, 0:n], nt_i[:, 0:n], nt_a[:, 0:n]
                link(dve.tensor_scalar(v, var, eps, None, ALU.add))
                link(dve.tensor_scalar(i0, v.bitcast(I32), 1, None, ALU.logical_shift_right))
                link(dve.tensor_scalar(out.bitcast(I32), i0, -1, MAGIC, ALU.mult, ALU.add))
                for _ in range(3):
                    link(dve.tensor_tensor(a, out, out, ALU.mult))
                    link(dve.scalar_tensor_tensor(a, a, -0.5, v, ALU.mult, ALU.mult))
                    link(dve.scalar_tensor_tensor(out, a, 1.5, out, ALU.add, ALU.mult))

            def norm_rows(dst, src, eps, n):
                passed(dve, ch.base)
                for g in range(n):
                    ins = dve.bn_stats(xstat[:, g, :], src(g))
                link(ins)
                passed(dve, ch.base)
                for g in range(n):
                    ins = dve.bn_aggr(xmv[:, g, :], xstat[:, g, :])
                link(ins)
                inv_sqrt(xrs[:, 0:n], xmv[:, 0:n, 1], eps, n)
                for g in range(n):
                    ins = dve.tensor_scalar(dst(g), src(g), xmv[:, g, 0:1], xrs[:, g:g + 1], ALU.subtract, ALU.mult)
                return ins

            def place(blk, src, done):
                for e in range(2):
                    for kp in range(2):
                        start = kp * 192 + 32 * e
                        ins = dve.tensor_copy(blk[64 * e:64 * e + 64, start:start + 3 * 257 + 1:257], src(e, kp))
                ins.then_inc(done, 1)

            dve.wait_ge(ld_vec, 16)
            dve.wait_ge(blk_zero, 3)
            place(NKblk, lambda e, kp: VEC[64 * e:64 * e + 64, V_NK:V_NK + 1].broadcast_to([64, 4]), nk_placed)
            dve.wait_ge(ld_x, 16)
            link(norm_rows(lambda g: rowtmp[:, g, :], lambda g: X[:, g, :], 1e-5, G))
            norm_rows(lambda g: rowtmp[:, g, :], lambda g: rowtmp[:, g, :], 1e-6, G).then_inc(x_normed, 1)

            def ctx_stats(g, k):
                passed(dve, g)
                for t in range(T):
                    src = CTX[:, GB * g + k, t, :] if isinstance(g, int) else col(CTX, g * GB + k)[:, t, :]
                    ins = dve.bn_stats(cstat[:, k * T + t, :], src)
                return ins

            def ctx_inv():
                passed(dve, ch.base)
                for n in range(GB * T):
                    ins = dve.bn_aggr(cmv[:, n, :], cstat[:, n, :])
                link(ins)
                inv_sqrt(crs[:, :], cmv[:, :, 1], 1e-6, GB * T)

            def ctx_apply(g, k):
                for t in range(T):
                    src = CTX[:, GB * g + k, t, :] if isinstance(g, int) else col(CTX, g * GB + k)[:, t, :]
                    n = k * T + t
                    ins = dve.tensor_scalar(NC[:, k, t, :], src, cmv[:, n, 0:1], crs[:, n:n + 1], ALU.subtract, ALU.mult)
                ins.then_inc(ctx_normed, 1)

            dve.wait_ge(xT_ready, 1)
            dve.tensor_scalar(xnT[:, :], pM[1][:, :], VEC[:, V_LN1S:V_LN1S + 1], VEC[:, V_LN1B:V_LN1B + 1],
                              ALU.mult, ALU.add).then_inc(xT_copied, 1)
            dve.wait_ge(vb_ready, 1)
            link(dve.tensor_scalar(nvk[:, :], pA[:, 0:KC], -1.0, VEC[:, V_NV:V_NV + 1], ALU.mult, ALU.add))
            place(NVblk, lambda e, kp: nvk[64 * e:64 * e + 64, kp:KC:2], nv_placed)
            dve.wait_ge(ld_ctx[0], 16)
            for k in range(GB):
                ins = ctx_stats(0, k)
            link(ins)
            ctx_inv()
            for k in range(GB):
                ctx_apply(0, k)
            dve.wait_ge(sn_copied, 1)
            link(dve.transpose(SNR[:, :, :].rearrange("p b g -> p (b g)"), sn_pad[:, :]))

            def mask_max(b, k):
                kk = k % 2
                dve.wait_ge(mask_ready, b + 1)
                if b_late(b):
                    dve.wait_ge(probsT_ready, b * T - T)
                for q in range(HG):
                    dve.wait_ge(scores_ready, b * HG + q + 1)
                    passed(dve, b)
                    ins = dve.tensor_tensor_reduce(SM[:, kk, q, :], pS[q % 2][:, :], MB[:, kk, :], 1.0, -BIG,
                                                   ALU.add, ALU.max, mrow[:, kk, q:q + 1])
                    ins.then_inc(masked, 1)
                dve.wait_ge(masked, b * HG + HG)
                null = col(SNR, b)[:, 0:HG]
                link(dve.tensor_tensor(mx4[:, :], mrow[:, kk, :], null, ALU.max))
                link(dve.tensor_scalar(negm[:, kk, :], mx4[:, :], -SCALE, None, ALU.mult))
                dve.scalar_tensor_tensor(snm[:, kk, :], null, SCALE, negm[:, kk, :], ALU.mult,
                                         ALU.add).then_inc(shift_ready, 1)

            def sums(b, k):
                kk = k % 2
                dve.wait_ge(exp_done, (b + 1) * (HG + 1))
                link(dve.tensor_tensor(lsum[:, :], rsum[:, kk, :], pn[:, kk, :], ALU.add))
                dve.reciprocal(rinv[:, kk, :], lsum[:, :]).then_inc(recip_ready, 1)
                dve.wait_ge(recip_ready, b + 1)
                link(dve.tensor_tensor(PNR[:, k % GB, 0:HG], pn[:, kk, :], rinv[:, kk, :], ALU.mult))

            def copy_pT(b, first=False):
                for t in (1, 3):
                    dve.wait_ge(probsT_ready, b * T + t + 1)
                    if t == 1 and not first:
                        dve.wait_ge(pv_ready, b)
                    dve.tensor_copy(PT[:, t, :], pP[t % 2][:, :]).then_inc(ptD_copied, 1)

            def copy_ac(b, k, it, first=False):
                dve.wait_ge(pv_ready, b + 1)
                if k == 0 and not first:
                    dve.wait_ge(out_ready, it)
                dve.tensor_scalar(AC[:, :, N * k:N * k + N], pA[:, :].rearrange("p (h i) -> p h i", h=H),
                                  VEC[:, V_LNCS:V_LNCS + 1], VEC[:, V_LNCB:V_LNCB + 1], ALU.mult,
                                  ALU.add).then_inc(ac_copied, 1)

            mask_max(0, 0)
            sums(0, 0)
            for g in range(1, G):
                dve.wait_ge(ld_ctx[g], 16)

            def body(it, first=False, last=False):
                for k in range(GB):
                    b = it * GB + k
                    if not (last and k == GB - 1):
                        mask_max(b + 1, k + 1)
                    copy_pT(b, first and k == 0)
                    if k == GB - 1:
                        if not first:
                            dve.wait_ge(out_ready, it)
                        link(dve.transpose(PNT[:, :], PNR[:, :, :].rearrange("p k g -> p (k g)")))
                        dve.sem_inc(pnT_ready, 1)
                    if not (last and k == GB - 1):
                        sums(b + 1, k + 1)
                    if not last and k < 2:
                        ctx_stats(it + 1, 2 * k)
                        link(ctx_stats(it + 1, 2 * k + 1))
                        if k == 1:
                            ctx_inv()
                    copy_ac(b, k, it, first)
                    if not last and k >= 1:
                        if k == 1:
                            ctx_apply(it + 1, 0)
                        ctx_apply(it + 1, k)

            ch.loop(0, 0)
            body(0, first=True)
            per_body = ch.n - ch.start
            ch.base = 0
            with dve.Fori(1, G - 1) as it:
                ch.loop(it - 1, per_body)
                body(it)
            ch.end(G - 2)
            body(G - 1, last=True)

            dve.wait_ge(ld_rows, 16)
            dve.wait_ge(out_copied, G)
            for b in range(GB):
                ins = dve.tensor_copy(kTe[:, b, N:LJ], VEC[:, V_BK:V_BK + 1])
            link(ins)
            with dve.Fori(0, G) as g:
                ch.loop(g, L_STEPS)
                xr = col(X, g)
                link(norm_rows(lambda _: y1[:, :], lambda _: col(OUT1, g), 1e-6, 1))
                link(dve.tensor_tensor(y1[:, :], y1[:, :], ROWS[:, 0, :], ALU.mult))
                link(dve.tensor_tensor(y1[:, :], y1[:, :], ROWS[:, 1, :], ALU.add))
                link(dve.tensor_tensor(xr, xr, y1[:, :], ALU.add))
                norm_rows(lambda _: xg[:, :], lambda _: xr, 1e-5, 1).then_inc(l_xn, 1)
                dve.wait_ge(l_q, g + 1)
                dve.tensor_scalar(qT[:, :], pM[0][:, 0:P], VEC[:, V_BQ:V_BQ + 1], LD ** -0.5, ALU.add,
                                  ALU.mult).then_inc(l_qc, 1)
                dve.wait_ge(l_k, g + 1)
                link(dve.tensor_scalar(kTe[:, :, 0:N], pM[1][:, 0:P].rearrange("p (b i) -> p b i", b=GB),
                                       VEC[:, V_BK:V_BK + 1], None, ALU.add))
                for r in range(LR):
                    ins = dve.tensor_scalar(Kbd[:, :, r, :], kTe[:, :, :], CON[:, K_R + r:K_R + r + 1], None, ALU.mult)
                ins.then_inc(l_kc, 1)
                dve.wait_ge(l_v, g + 1)
                dve.tensor_tensor(Vbd[:, :, :], pA[:, :].rearrange("p (b c) -> p b c", b=GB),
                                  CON[:, K_V:K_V + C].unsqueeze(1).broadcast_to([P, GB, C]), ALU.mult).then_inc(l_vc, 1)
                dve.wait_ge(l_s, g + 1)
                banks = [pS[0], pS[1], pP[0], pP[1]]
                for r in range(4):
                    ins = dve.tensor_reduce(lmax[:, 4 * r:4 * r + 4],
                                            banks[r][:, 0:LR * LJ].rearrange("p (h j) -> p h j", h=LR), AX.X, ALU.max)
                link(ins)
                for r in range(4):
                    ins = dve.tensor_tensor(SL[:, 4 * r:4 * r + 4, :],
                                            banks[r][:, 0:LR * LJ].rearrange("p (h j) -> p h j", h=LR),
                                            lmax[:, 4 * r:4 * r + 4].unsqueeze(2).broadcast_to([P, LR, LJ]),
                                            ALU.subtract)
                ins.then_inc(l_sub, 1)
                dve.wait_ge(l_exp, g + 1)
                link(dve.tensor_scalar(SL[:, :, N:LJ], SL[:, :, N:LJ], float(PADS), None, ALU.mult))
                link(dve.tensor_reduce(lden[:, :], SL[:, :, :], AX.X, ALU.add))
                link(dve.reciprocal(lrec[:, :], lden[:, :]))
                dve.tensor_tensor(PL[:, :, :], SL[:, :, 0:N], lrec[:, :].unsqueeze(2).broadcast_to([P, 16, N]),
                                  ALU.mult).then_inc(l_p, 1)
                dve.wait_ge(l_o, g + 1)
                dve.tensor_scalar(oT[:, :], pM[0][:, 0:P], VEC[:, V_BV:V_BV + 1], None, ALU.add).then_inc(l_oc, 1)
                dve.wait_ge(l_y, g + 1)
                link(dve.tensor_tensor(xr, xr, pM[1][:, 0:C], ALU.add))
                link(dve.tensor_tensor(xr, xr, ROWS[:, 2, :], ALU.add))
            ch.end(G)

            norm_rows(lambda g: fn[:, g, :], lambda g: X[:, g, :], 1e-5, G).then_inc(f_n, 1)
            dve.tensor_scalar(b1v[:, :, :], VEC[:, V_B1:V_B1 + 4 * E].rearrange("p (e v i) -> p e v i", v=2, i=2)[:, :, 1, :],
                              1.0, None, ALU.add)
            dve.wait_ge(f_g, 1)
            link(dve.tensor_copy(gt[:, :, :].rearrange("p g e -> p (g e)"), pP[0][:, 0:G * E]))

            def bc(t):
                return t[:, :].unsqueeze(2).broadcast_to([P, G, E])

            def first_best(src, m, one_hot):
                link(dve.tensor_reduce(m[:, :], src[:, :, :], AX.X, ALU.max))
                link(dve.tensor_tensor(g_a[:, :, :], src[:, :, :], bc(m), ALU.is_equal))
                link(dve.tensor_tensor(g_a[:, :, :], g_a[:, :, :],
                                       CON[:, K_IOTA:K_IOTA + E].unsqueeze(1).broadcast_to([P, G, E]), ALU.mult))
                link(dve.tensor_reduce(gi[:, :], g_a[:, :, :], AX.X, ALU.max))
                link(dve.tensor_tensor(one_hot[:, :, :], g_a[:, :, :], bc(gi), ALU.is_equal))

            first_best(gt, gm1, g_is1)
            link(dve.scalar_tensor_tensor(g_rest[:, :, :], g_is1[:, :, :], -BIG, gt[:, :, :], ALU.mult, ALU.add))
            first_best(g_rest, gm2, g_is2)
            dve.tensor_tensor(gd[:, :], gm2[:, :], gm1[:, :], ALU.subtract).then_inc(f_gd, 1)
            dve.wait_ge(f_ge, 1)
            link(dve.tensor_scalar(gp1[:, :], gp2[:, :], 1.0, None, ALU.add))
            link(dve.reciprocal(gp1[:, :], gp1[:, :]))
            link(dve.tensor_tensor(gp2[:, :], gp2[:, :], gp1[:, :], ALU.mult))
            link(dve.tensor_tensor(g_is1[:, :, :], g_is1[:, :, :], bc(gp1), ALU.mult))
            link(dve.tensor_tensor(g_is2[:, :, :], g_is2[:, :, :], bc(gp2), ALU.mult))
            link(dve.tensor_tensor(gw[:, :, :], g_is1[:, :, :], g_is2[:, :, :], ALU.add))
            dve.sem_inc(f_w, 1)
            dve.wait_ge(f_b, 1)
            dve.tensor_tensor(X[:, :, :].rearrange("p g c -> p (g c)"), X[:, :, :].rearrange("p g c -> p (g c)"),
                              pA[:, :], ALU.add).then_inc(e_yc, 1)

            def clip(e):
                for i in range(2):
                    dve.wait_ge(e_h, e * 2 + i + 1)
                    bias = VEC[:, bass.ds(e * 4 + V_B1 + i, 1)]
                    dve.tensor_scalar(hg[:, i, :], (pS, pP)[i][0][:, :], bias, 9.0, ALU.add, ALU.min)
                    dve.tensor_scalar(hv[:, i, :], (pS, pP)[i][1][:, :], col(b1v, e)[:, i:i + 1], -8.0, ALU.add,
                                      ALU.max).then_inc(e_hc, 1)

            def swiglu(e, first=False):
                for i in range(2):
                    dve.wait_ge(e_sg, e * 2 + i + 1)
                    if i == 0 and not first:
                        dve.wait_ge(e_y, e)
                    dve.scalar_tensor_tensor(hT[:, i, :], hv[:, i, :], 10.0, hs[:, i, :], ALU.min,
                                             ALU.mult).then_inc(e_hT, 1)

            def add_expert(e):
                dve.wait_ge(e_y, e + 1)
                dve.wait_ge(e_yc, e + 1)
                for g in range(G):
                    ins = dve.scalar_tensor_tensor(X[:, g, :], pA[:, g * C:(g + 1) * C], gw[:, g, bass.ds(e, 1)],
                                                   X[:, g, :], ALU.mult, ALU.add)
                ins.then_inc(e_yc, 1)

            clip(0)
            dve.wait_ge(e_hc, 2)
            swiglu(0, True)
            with dve.Fori(0, E - 1) as e:
                dve.wait_ge(e_hT, e * 2 + 2)
                clip(e + 1)
                add_expert(e)
                dve.wait_ge(e_hc, e * 2 + 4)
                swiglu(e + 1)
            add_expert(E - 1)


def kernel(**inputs):
    import numpy as np
    import concourse.bacc as bacc
    from concourse.bass_utils import run_bass_kernel_spmd as run

    a = {n: np.asarray(v) for n, v in inputs.items()}
    wq, wkv, wo = a["L0_xattn_Wq"], a["L0_xattn_Wkv"], a["L0_xattn_Wo"]
    nk, nv = a["L0_xattn_null_kv"]
    bqkv = a["L0_attn_b_qkv"].reshape(3, C)
    b1 = a["L0_ffn_dense_1_b"].reshape(E, 2, P, 2).transpose(2, 0, 3, 1).reshape(P, 4 * E)
    vec = np.concatenate([np.stack([a["L0_xattn_ln1_s"], a["L0_xattn_ln1_b"], a["L0_xattn_lnc_s"], a["L0_xattn_lnc_b"],
                                    bqkv[0], bqkv[1], bqkv[2], np.concatenate([nk, nk]), np.concatenate([nv, nv])],
                                   axis=1), b1], axis=1)
    rows = np.stack([a["L0_xattn_lno_s"], a["L0_xattn_lno_b"], a["L0_attn_b_out"]])[None]
    ch = np.arange(P)
    const = np.zeros((P, K_COLS), np.float32)
    const[:, K_ID:K_ID + P] = np.eye(P)
    const[:, K_R:K_R + LR] = (ch[:, None] // LD) % LR == np.arange(LR)[None]
    const[:, K_V:K_V + C] = ch[:, None] // N == (ch[None] // LD) % LR
    const[:, K_IOTA:K_IOTA + E] = E - np.arange(E)
    w1 = a["L0_ffn_dense_1_w"].reshape(E, 2, P, 2, C).transpose(0, 4, 3, 1, 2)
    w2 = a["L0_ffn_dense_2_w"].reshape(E, C, 2, P).transpose(0, 3, 2, 1)
    mask = a["mask_BxS2_bf1"].view(np.uint8).reshape(B, P, T).transpose(0, 2, 1).reshape(1, B * M)
    arrays = {
        "x": a["x"].reshape(B * N, C), "ctx_in": a["ctx_1024"].reshape(B * M, C), "mask": mask, "vec": vec,
        "rows": rows, "const": const, "wqT": wq.T, "wkT": wkv[:, :H * D].T, "wvT": wkv[:, H * D:].T,
        "wv": wkv[:, H * D:], "wo": wo, "wqkv": a["L0_attn_w_qkv"], "wout": a["L0_attn_w_out"],
        "gate": a["L0_ffn_gate_w"], "w1": w1, "w2": w2, "b2": a["L0_ffn_dense_2_b"],
    }
    arrays = {f"{n}_dram": np.ascontiguousarray(v) for n, v in arrays.items()}
    nc = bacc.Bacc("TRN2", target_bir_lowering=False, num_devices=1)
    aps = [nc.dram_tensor(n, v.shape, mybir.dt.from_np(v.dtype), kind="ExternalInput").ap() for n, v in arrays.items()]
    out = nc.dram_tensor("out_dram", (B * N, C), F32, kind="ExternalOutput").ap()
    perceiver(nc, *aps, out)
    result = run(nc, [arrays], core_ids=[0])
    return result.results[0]["out_dram"].reshape(B, N, C)
```

```python
from contextlib import ExitStack

import concourse.bass as bass
from concourse import mybir

ALU = mybir.AluOpType
ACT = mybir.ActivationFunctionType
AX = mybir.AxisListType
F32 = mybir.dt.float32
I32 = mybir.dt.int32
BF16 = mybir.dt.bfloat16
U8 = mybir.dt.uint8

P = 128
B, N, C = 16, 32, 128
M = 512
H, D = 16, 64
GB = P // N
G = B // GB
T = M // P
HG = H // GB
KC = H * D // P
LD = C // 16
LR = 32 // LD
LJ = N + 1
PADS = 64 - N
E = 8
EB = 4
BODY_STEPS = 87
SCALE = H ** -0.5
BIG = 3e38
MAGIC = 0x5F3759DF

V_LN1S, V_LN1B, V_LNCS, V_LNCB, V_BQ, V_BK, V_BV, V_NK, V_NV = range(9)
V_B1 = 9
V_N = V_B1 + E * 4
K_ID, K_R, K_V, K_N = 0, P, P + LR, 2 * P + LR
K_IOTA = K_N
K_COLS = K_N + E


def at(t, i):
    return t[i] if isinstance(i, int) else t[bass.ds(i, 1)].squeeze(0)


def col(t, i):
    return t[:, i] if isinstance(i, int) else t[:, bass.ds(i, 1)].squeeze(1)


class Chain:

    def __init__(self, eng, sem):
        self.eng, self.sem, self.n, self.base = eng, sem, 0, 0

    def link(self, ins):
        ins.then_inc(self.sem, 1)
        self.n += 1
        self.eng.wait_ge(self.sem, self.base + self.n)

    def loop(self, it, per_body):
        self.start = self.n
        self.base = it * per_body
        self.per_body = per_body

    def end(self, times):
        assert self.n - self.start == self.per_body, (self.n - self.start, self.per_body)
        self.n += (times - 1) * self.per_body
        self.base = 0


def perceiver(nc, x, ctx_in, mask, vec, rows, const, wqT, wkT, wvT, wv, wo, wqkv, wout, gate, w1, w2, b2, out):
    with ExitStack() as ctx:
        def sb(name, shape, dt=F32):
            return ctx.enter_context(nc.sbuf_tensor(name, shape, dt))

        def ps(name, shape=(P, 512)):
            return ctx.enter_context(nc.psum_tensor(name, list(shape), F32))

        def sem(name):
            return ctx.enter_context(nc.semaphore(name))

        X = sb("X", [P, G, C])
        VEC = sb("VEC", [P, V_N])
        ROWS = sb("ROWS", [P, 3, C])
        CON = sb("CON", [P, K_COLS])
        WqT = sb("WqT", [P, KC, C])
        WkT = sb("WkT", [P, KC, C])
        WvT = sb("WvT", [P, KC, C])
        Wv = sb("Wv", [P, H * D])
        Wo = sb("Wo", [P, KC, C])
        Wqkv = sb("Wqkv", [P, 3 * C])
        Wout = sb("Wout", [P, C])
        Gate = sb("Gate", [P, E])
        B2 = sb("B2", [E, C])
        CTX = sb("CTX", [P, B, T, C])
        MK8 = sb("MK8", [P, B, M], U8)
        MB = sb("MB", [P, 2, M], BF16)
        A = sb("A", [P, H, C])
        Bm = sb("Bm", [P, H, C])
        U = sb("U", [P, P])
        NVW = sb("NVW", [P, C])
        NKblk = sb("NKblk", [P, KC * P])
        NVblk = sb("NVblk", [P, KC * P])
        nvk = sb("nvk", [P, KC])
        xnT = sb("xnT", [P, G * P])
        sn_pad = sb("sn_pad", [P, G * P])
        SNR = sb("SNR", [P, B, N])
        rowtmp = sb("rowtmp", [P, G, C])

        NC = sb("NC", [P, GB, T, C])
        cnT = sb("cnT", [P, 2, M])
        QK = sb("QK", [P, GB, H, N])
        SM = sb("SM", [P, GB, HG, M])
        PT = sb("PT", [P, T, M])
        AC = sb("AC", [P, H, P])
        PNR = sb("PNR", [P, GB, N])
        PNT = sb("PNT", [P, P])
        OUT1 = sb("OUT1", [P, C])
        cstat = sb("cstat", [P, GB * T, 6])
        cmv = sb("cmv", [P, GB * T, 2])
        crs = sb("crs", [P, GB * T])
        mrow = sb("mrow", [P, GB, HG])
        mx4 = sb("mx4", [P, HG])
        negm = sb("negm", [P, GB, HG])
        snm = sb("snm", [P, GB, HG])
        rsum = sb("rsum", [P, GB, HG])
        pn = sb("pn", [P, GB, HG])
        lsum = sb("lsum", [P, HG])
        rinv = sb("rinv", [P, GB, HG])
        xstat = sb("xstat", [P, G, 6])
        xmv = sb("xmv", [P, G, 2])
        xrs = sb("xrs", [P, G])
        nt_v = sb("nt_v", [P, GB * T])
        nt_i = sb("nt_i", [P, GB * T], I32)
        nt_a = sb("nt_a", [P, GB * T])

        y1 = sb("y1", [P, C])
        xg = sb("xg", [P, C])
        xgT = sb("xgT", [P, P])
        XR = sb("XR", [P, GB, LR, N])
        qT = sb("qT", [P, P])
        kTe = sb("kTe", [P, GB, LJ])
        Kbd = sb("Kbd", [P, GB, LR, LJ])
        Vbd = sb("Vbd", [P, GB, C])
        SL = sb("SL", [P, 16, LJ])
        PL = sb("PL", [P, 16, N])
        PLT = sb("PLT", [P, 4, P])
        lmax = sb("lmax", [P, 16])
        lden = sb("lden", [P, 16])
        lrec = sb("lrec", [P, 16])
        oT = sb("oT", [P, P])

        fn = sb("fn", [P, G, C])
        fnT = sb("fnT", [P, G * P])
        gt = sb("gt", [P, G, E])
        g_is1 = sb("g_is1", [P, G, E])
        g_a = sb("g_a", [P, G, E])
        g_rest = sb("g_rest", [P, G, E])
        g_is2 = sb("g_is2", [P, G, E])
        gw = sb("gw", [P, G, E])
        gm1 = sb("gm1", [P, G])
        gm2 = sb("gm2", [P, G])
        gi = sb("gi", [P, G])
        gd = sb("gd", [P, G])
        gp1 = sb("gp1", [P, G])
        gp2 = sb("gp2", [P, G])
        gwT = sb("gwT", [E, G * P])
        b1v = sb("b1v", [P, E, 2])
        W1s = [sb(f"W1s{i}", [P, 2, 2, P]) for i in range(EB)]
        W2s = [sb(f"W2s{i}", [P, 2, C]) for i in range(EB)]
        hg, hv, hs, hT = SM[:, 0, 0:2, :], SM[:, 0, 2:4, :], SM[:, 1, 0:2, :], SM[:, 1, 2:4, :]

        pS = [ps("pS0"), ps("pS1")]
        pP = [ps("pP0"), ps("pP1")]
        pA, pC = ps("pA"), ps("pC")
        pM = [ps("pM0"), ps("pM1")]

        ld_x, ld_vec, ld_con, ld_rows = sem("ld_x"), sem("ld_vec"), sem("ld_con"), sem("ld_rows")
        ld_wq, ld_wk, ld_wvT, ld_wv, ld_wo = sem("ld_wq"), sem("ld_wk"), sem("ld_wvT"), sem("ld_wv"), sem("ld_wo")
        ld_ctx = [sem(f"ld_ctx{g}") for g in range(G)]
        ld_mask = sem("ld_mask")
        ld_loc, ld_wl = sem("ld_loc"), sem("ld_wl")
        ld_e = [sem(f"ld_e{i}") for i in range(EB)]
        dve_step, act_step, pool_step, pe_step = sem("dve_step"), sem("act_step"), sem("pool_step"), sem("pe_step")
        mask_copied = sem("mask_copied")
        mask_ready = sem("mask_ready")
        wait_passed = {e.engine: sem(f"wait_passed_{n}") for n, e in
                       (("dve", nc.vector), ("pe", nc.tensor), ("pool", nc.gpsimd))}
        blk_zero = sem("blk_zero")
        x_normed, xT_ready, xT_copied = sem("x_normed"), sem("xT_ready"), sem("xT_copied")
        nk_placed, u_ready, u_copied = sem("nk_placed"), sem("u_ready"), sem("u_copied")
        vb_ready, nv_placed, nvw_ready, nvw_copied = sem("vb_ready"), sem("nv_placed"), sem("nvw_ready"), sem("nvw_copied")
        wA_ready, wA_copied = sem("wA_ready"), sem("wA_copied")
        wB_ready, wB_copied = sem("wB_ready"), sem("wB_copied")
        masked = sem("masked")
        sn_ready, sn_copied, sn_rows = sem("sn_ready"), sem("sn_copied"), sem("sn_rows")
        ctx_normed, cT_ready, cT_copied = sem("ctx_normed"), sem("cT_ready"), sem("cT_copied")
        qk_ready, qk_copied = sem("qk_ready"), sem("qk_copied")
        scores_ready, shift_ready, exp_done = sem("scores_ready"), sem("shift_ready"), sem("exp_done")
        probs_normed = sem("probs_normed")
        probsT_ready, pt_copied = sem("probsT_ready"), sem("pt_copied")
        pv_ready, ac_copied, pnT_ready = sem("pv_ready"), sem("ac_copied"), sem("pnT_ready")
        out_ready, out_copied = sem("out_ready"), sem("out_copied")
        l_xn, l_xT, l_xTc = sem("l_xn"), sem("l_xT"), sem("l_xTc")
        l_q, l_k, l_v = sem("l_q"), sem("l_k"), sem("l_v")
        l_qc, l_kc, l_vc = sem("l_qc"), sem("l_kc"), sem("l_vc")
        l_s, l_sub, l_exp, l_p, l_pT, l_pTc = (sem("l_s"), sem("l_sub"), sem("l_exp"), sem("l_p"), sem("l_pT"),
                                               sem("l_pTc"))
        l_s1 = sem("l_s1")
        l_o, l_oc, l_y, l_yc = sem("l_o"), sem("l_oc"), sem("l_y"), sem("l_yc")
        f_n, f_T, f_Tc, f_g, f_gd, f_ge, f_w, f_wT, f_wTc, f_b, f_bc = (
            sem(f"f_{n}") for n in ("n", "T", "Tc", "g", "gd", "ge", "w", "wT", "wTc", "b", "bc"))
        e_h, e_hc, e_sg, e_hT, e_y, e_yc = (sem(f"e_{n}") for n in ("h", "hc", "sg", "hT", "y", "yc"))
        x1_ready, x2_ready, st_out = sem("x1_ready"), sem("x2_ready"), sem("st_out")

        def passed(eng, i):
            if not isinstance(i, int):
                eng.sem_inc(wait_passed[eng.engine], 1)

        ident = CON[:, K_ID:K_ID + P]
        block = ctx.enter_context(nc.Block())

        @block.sync
        def _(sp):
            sp.dma_start(X[:, :, :], x.rearrange("(g p) c -> p g c", p=P)).then_inc(ld_x, 16)
            sp.dma_start(VEC[:, :], vec).then_inc(ld_vec, 16)
            sp.dma_start(CON[:, :], const).then_inc(ld_con, 16)
            sp.dma_start(WqT[:, :, :], wqT.rearrange("(k p) c -> p k c", p=P)).then_inc(ld_wq, 16)
            sp.dma_start(WkT[:, :, :], wkT.rearrange("(k p) c -> p k c", p=P)).then_inc(ld_wk, 16)
            for g in range(G):
                sp.dma_start(CTX[:, GB * g:GB * (g + 1), :, :],
                             ctx_in[GB * g * M:GB * (g + 1) * M, :].rearrange("(b p t) c -> p b t c", p=P, t=T)
                             ).then_inc(ld_ctx[g], 16)
                if g == 0:
                    sp.dma_start(Wv[:, :], wv).then_inc(ld_wv, 16)
                    sp.dma_start(WvT[:, :, :], wvT.rearrange("(k p) c -> p k c", p=P)).then_inc(ld_wvT, 16)
                    sp.dma_start(Wo[:, :, :], wo.rearrange("(k p) c -> p k c", p=P)).then_inc(ld_wo, 16)
            sp.dma_start(ROWS[:, :, :], rows.broadcast_to([P, 3, C])).then_inc(ld_rows, 16)
            sp.dma_start(Wqkv[:, :], wqkv).then_inc(ld_loc, 16)
            sp.dma_start(Wout[:, :], wout).then_inc(ld_loc, 16)
            sp.dma_start(Gate[:, :], gate).then_inc(ld_loc, 16)
            sp.dma_start(B2[:, :], b2).then_inc(ld_loc, 16)
            for e in range(E):
                if e >= EB:
                    sp.wait_ge(e_y, e - EB + 1)
                sp.dma_start(W1s[e % EB][:, :, :, :], w1[e]).then_inc(ld_e[e % EB], 16)
                sp.dma_start(W2s[e % EB][:, :, :], w2[e]).then_inc(ld_e[e % EB], 16)
            sp.wait_ge(e_yc, E + 1)
            sp.dma_start(out.rearrange("(g p) c -> p g c", p=P), X[:, :, :]).then_inc(st_out, 16)
            sp.wait_ge(st_out, 16)

        @block.gpsimd
        def _(pool):
            pool.memset(NKblk[:, :], 0.0).then_inc(blk_zero, 1)
            pool.memset(NVblk[:, :], 0.0).then_inc(blk_zero, 1)
            pool.memset(PNR[:, :, :], 0.0).then_inc(blk_zero, 1)

            def mask_bias(b, k):
                pool.tensor_copy(MB[:, k, :], col(MK8, b)).then_inc(mask_copied, 1)
                pool.wait_ge(mask_copied, b + 1)
                passed(pool, b)
                pool.tensor_scalar(MB[:, k, :], MB[:, k, :], BIG, -BIG, ALU.mult, ALU.add).then_inc(mask_ready, 1)

            pool.wait_ge(ld_mask, 16)
            mask_bias(0, 0)
            mask_bias(1, 1)

            with pool.Fori(1, B // 2) as it:
                for k in range(2):
                    pool.wait_ge(masked, (it * 2 + k - 1) * HG)
                    mask_bias(it * 2 + k, k)

        @block.scalar
        def _(act):
            act.dma_start(MK8[:, :, :].rearrange("p b m -> p (b m)"), mask.broadcast_to([P, B * M])).then_inc(ld_mask, 16)

            def copy_cT(b, k, first=False):
                act.wait_ge(cT_ready, b + 1)
                if not first:
                    act.wait_ge(scores_ready, b * HG - HG)
                act.activation(cnT[:, k % 2, :], pC[:, :], ACT.Identity, bias=VEC[:, V_LNCB:V_LNCB + 1],
                               scale=VEC[:, V_LNCS:V_LNCS + 1]).then_inc(cT_copied, 1)

            def copy_qk(g, first=False):
                for q in range(HG):
                    act.wait_ge(qk_ready, g * HG + q + 1)
                    if q == 0 and not first:
                        act.wait_ge(scores_ready, g * GB * HG)
                    act.copy(QK[:, :, GB * q:GB * (q + 1), :].rearrange("p k h i -> p h k i"),
                             pM[q % 2][:, :].rearrange("p (h k i) -> p h k i", h=GB, k=GB)).then_inc(qk_copied, 1)

            def exps(b, k):
                act.wait_ge(shift_ready, b + 1)
                act.activation(pn[:, k, :], snm[:, k, :], ACT.Exp).then_inc(exp_done, 1)
                for q in range(HG):
                    act.activation(SM[:, k, q, :], SM[:, k, q, :], ACT.Exp, bias=negm[:, k, q:q + 1],
                                   scale=SCALE, accum_out=rsum[:, k, q:q + 1]).then_inc(exp_done, 1)

            def copy_pT(b, first=False):
                for t in range(T):
                    act.wait_ge(probsT_ready, b * T + t + 1)
                    if t == 0 and not first:
                        act.wait_ge(pv_ready, b)
                    act.copy(PT[:, t, :], pP[t % 2][:, :]).then_inc(pt_copied, 1)

            def copy_ac(b, k, reads=None):
                act.wait_ge(pv_ready, b + 1)
                if reads is not None:
                    act.wait_ge(out_ready, reads)
                act.activation(AC[:, :, N * k:N * k + N], pA[:, :].rearrange("p (h i) -> p h i", h=H), ACT.Identity,
                               bias=VEC[:, V_LNCB:V_LNCB + 1], scale=VEC[:, V_LNCS:V_LNCS + 1]).then_inc(ac_copied, 1)

            def copy_out(g):
                act.wait_ge(out_ready, g + 1)
                act.copy(OUT1[:, :], pC[:, 0:C]).then_inc(out_copied, 1)

            def copy_xgT(g):
                act.wait_ge(l_xT, g + 1)
                act.copy(xgT[:, :], pC[:, 0:P])
                act.copy(XR[:, :, :, :], pC[:, 0:P].rearrange("p (b i) -> p b i", b=GB).unsqueeze(2)
                         .broadcast_to([P, GB, LR, N])).then_inc(l_xTc, 1)

            def local_exp(g):
                act.wait_ge(l_sub, g + 1)
                act.activation(SL[:, :, :], SL[:, :, :], ACT.Exp).then_inc(l_exp, 1)

            def copy_plT(g):
                act.wait_ge(l_pT, g + 1)
                act.copy(PLT[:, :, :].rearrange("p a b -> p (a b)"), pM[0][:, :]).then_inc(l_pTc, 1)

            def copy_heads(W, q, done):
                for e in range(2):
                    ins = act.copy(W[:, 4 * q + e:4 * q + 4:2, :],
                                   (pP, pS)[q % 2][e][:, 0:2 * C].rearrange("p (a c) -> p a c", a=2))
                ins.then_inc(done, 1)

            act.wait_ge(u_ready, 1)
            act.copy(U[:, :], pC[:, 0:P]).then_inc(u_copied, 1)
            for q in range(H // 4):
                act.wait_ge(wA_ready, q + 1)
                copy_heads(A, q, wA_copied)
            act.wait_ge(sn_ready, 1)
            act.copy(sn_pad[:, :], pM[0][:, :]).then_inc(sn_copied, 1)
            copy_qk(0, True)
            for q in range(H // 4):
                act.wait_ge(wB_ready, q + 1)
                copy_heads(Bm, q, wB_copied)
            act.wait_ge(nvw_ready, 1)
            act.copy(NVW[:, :], pC[:, 0:C]).then_inc(nvw_copied, 1)
            act.wait_ge(ld_vec, 16)
            copy_cT(0, 0, True)
            copy_cT(1, 1, True)
            exps(0, 0)
            copy_cT(2, 2)

            def body(it, first=False, last=False):
                for k in range(GB):
                    b = it * GB + k
                    if not (first and k == 0):
                        copy_ac(b - 1, (k - 1) % GB, it if k == 1 and not first else None)
                    if not (last and k == GB - 1):
                        exps(b + 1, (k + 1) % GB)
                    if k == 0 and not first:
                        copy_out(it - 1)
                    if k == 1 and not first:
                        copy_xgT(it - 1)
                    if k == 1 and not last:
                        copy_qk(it + 1)
                    if k == 3 and not first:
                        copy_plT(it - 1)
                    copy_pT(b, first and k == 0)
                    if not (last and k > 0):
                        copy_cT(b + 3, k + 1)
                    if k == 2 and not first:
                        local_exp(it - 1)

            body(0, first=True)
            with act.Fori(1, G - 1) as it:
                body(it)
            body(G - 1, last=True)
            copy_ac(B - 1, GB - 1)
            for stage in (copy_out, copy_xgT, local_exp, copy_plT):
                stage(G - 1)

            act.wait_ge(f_T, 1)
            act.copy(fnT[:, :], pC[:, :]).then_inc(f_Tc, 1)
            act.wait_ge(f_gd, 1)
            act.activation(gp2[:, :], gd[:, :], ACT.Exp).then_inc(f_ge, 1)
            act.wait_ge(f_wT, 1)
            act.copy(gwT[:, :], pP[1][0:E, :]).then_inc(f_wTc, 1)
            with act.Fori(0, E) as e:
                for i in range(2):
                    act.wait_ge(e_hc, e * 2 + i + 3)
                    act.activation(hs[:, i, :], hg[:, i, :], ACT.Gelu_apprx_sigmoid).then_inc(e_sg, 1)

        @block.tensor
        def _(pe):
            def head_products(L, R, q, done):
                for a in range(2):
                    for e in range(2):
                        ins = pe.matmul((pP, pS)[q % 2][e][:, a * C:(a + 1) * C], L[64 * e:64 * e + 64, 2 * q + a, :],
                                        R[64 * e:64 * e + 64, 2 * q + a, :], start=True, stop=True)
                ins.then_inc(done, 1)

            pe.wait_ge(ld_wq, 16)
            pe.wait_ge(nk_placed, 1)
            for c in range(KC):
                ins = pe.matmul(pC[:, 0:P], WqT[:, c, :], NKblk[:, c * P:(c + 1) * P], start=(c == 0), stop=(c == KC - 1))
            ins.then_inc(u_ready, 1)
            pe.wait_ge(ld_wk, 16)
            for q in range(H // 4):
                if q >= 2:
                    pe.wait_ge(wA_copied, q - 1)
                head_products(WqT, WkT, q, wA_ready)
            pe.wait_ge(x_normed, 1)
            pe.wait_ge(ld_con, 16)
            for g in range(G):
                ins = pe.transpose(pM[1][:, g * P:(g + 1) * P], rowtmp[:, g, :], ident)
            ins.then_inc(xT_ready, 1)
            pe.wait_ge(xT_copied, 1)
            pe.wait_ge(u_copied, 1)
            pe.matmul(pM[0][:, :], U[:, :], xnT[:, :], start=True, stop=True).then_inc(sn_ready, 1)

            def qk(g, first=False):
                for q in range(HG):
                    if not (first and q < 2):
                        pe.wait_ge(qk_copied, g * HG + q - 1)
                    for h in range(4):
                        ins = pe.matmul(pM[q % 2][:, h * P:(h + 1) * P], A[:, 4 * q + h, :],
                                        xnT[:, bass.ds(g * P, P)], start=True, stop=True)
                    ins.then_inc(qk_ready, 1)

            def ctx_T(b, k, first=False):
                pe.wait_ge(ctx_normed, b + 1)
                if not first:
                    pe.wait_ge(cT_copied, b)
                for t in range(T):
                    ins = pe.transpose(pC[:, t * P:(t + 1) * P], NC[:, k, t, :], ident)
                ins.then_inc(cT_ready, 1)

            def scores(b, k, g, first=False):
                pe.wait_ge(cT_copied, b + 1)
                if k == 0:
                    pe.wait_ge(qk_copied, g * HG + HG)
                for q in range(HG):
                    if not (first and q < 2):
                        pe.wait_ge(masked, b * HG + q - 1)
                    pe.matmul(pS[q % 2][:, :], QK[:, k, 4 * q:4 * q + 4, :].rearrange("p h i -> p (h i)"),
                              cnT[:, k % 2, :], start=True, stop=True).then_inc(scores_ready, 1)

            def probs_T(b, k, t, first=False):
                if t == 0:
                    pe.wait_ge(probs_normed, b * HG + HG)
                if not (first and t < 2):
                    pe.wait_ge(pt_copied, b * T + t - 1)
                for q in range(HG):
                    ins = pe.transpose(pP[t % 2][:, q * P:(q + 1) * P], SM[:, k, q, t * P:(t + 1) * P], ident)
                ins.then_inc(probsT_ready, 1)

            def pv(b, k, t, first=False):
                if t == 0 and not first:
                    pe.wait_ge(ac_copied, b)
                pe.wait_ge(pt_copied, b * T + t + 1)
                ins = pe.matmul(pA[:, :], NC[:, k, t, :], PT[:, t, :], start=(t == 0), stop=(t == T - 1))
                if t == T - 1:
                    ins.then_inc(pv_ready, 1)

            pe.wait_ge(ld_wv, 16)
            pe.wait_ge(ld_vec, 16)
            for c in range(KC):
                ins = pe.matmul(pA[:, c:c + 1], Wv[:, c * P:(c + 1) * P], VEC[:, V_LNCB:V_LNCB + 1], start=True, stop=True)
            ins.then_inc(vb_ready, 1)
            pe.wait_ge(sn_copied, 1)
            pe.wait_ge(wA_copied, H // 4)
            qk(0, True)
            pe.wait_ge(ld_wvT, 16)
            pe.wait_ge(ld_wo, 16)
            for q in range(H // 4):
                if q >= 2:
                    pe.wait_ge(wB_copied, q - 1)
                head_products(WvT, Wo, q, wB_ready)
            pe.wait_ge(nv_placed, 1)
            for c in range(KC):
                ins = pe.matmul(pC[:, 0:C], NVblk[:, c * P:(c + 1) * P], Wo[:, c, :], start=(c == 0), stop=(c == KC - 1))
            ins.then_inc(nvw_ready, 1)
            pe.wait_ge(nvw_copied, 1)
            pe.wait_ge(wB_copied, H // 4)
            ctx_T(0, 0, True)
            scores(0, 0, 0, True)
            ctx_T(1, 1)
            scores(1, 1, 0)
            ctx_T(2, 2)

            def project(g, contexts):
                pe.wait_ge(cT_copied, contexts)
                pe.wait_ge(pnT_ready, g + 1)
                pe.wait_ge(ac_copied, g * GB + GB)
                for h in range(H):
                    pe.matmul(pC[:, 0:C], AC[:, h, :], Bm[:, h, :], start=(h == 0), stop=False)
                pe.matmul(pC[:, 0:C], PNT[:, :], NVW[:, :], start=False, stop=True).then_inc(out_ready, 1)

            def local_T(g, contexts):
                pe.wait_ge(cT_copied, contexts)
                pe.wait_ge(l_xn, g + 1)
                pe.transpose(pC[:, 0:P], xg[:, :], ident).then_inc(l_xT, 1)

            def local_qkv(g):
                pe.wait_ge(l_xTc, g + 1)
                pe.matmul(pM[0][:, 0:P], Wqkv[:, 0:C], xgT[:, :], start=True, stop=True)
                pe.matmul(pM[0][:, P:2 * P], Wqkv[:, C:2 * C], xgT[:, :], start=True, stop=True).then_inc(l_k, 1)
                for b in range(GB):
                    ins = pe.matmul(pM[1][:, b * C:(b + 1) * C], XR[:, b, :, :].rearrange("p r i -> p (r i)"),
                                    Wqkv[:, 2 * C:3 * C], start=True, stop=True)
                ins.then_inc(l_v, 1)

            def local_scores(g):
                pe.wait_ge(l_kc, g + 1)
                pe.wait_ge(l_vc, g + 1)
                passed(pe, g)
                for half in range(2):
                    for b in range(GB):
                        for bank in range(2):
                            r = 2 * bank + half
                            ins = pe.matmul(pM[bank][N * b:N * b + N, half * LR * LJ:(half + 1) * LR * LJ],
                                            qT[32 * r:32 * r + 32, N * b:N * b + N],
                                            Kbd[32 * r:32 * r + 32, b, :, :].rearrange("p r j -> p (r j)"),
                                            start=True, stop=True)
                    ins.then_inc(l_s1, 1)
                    if half == 0:
                        pe.wait_ge(l_s1, g * 2 + 1)
                        passed(pe, g)

            def local_pT(g):
                pe.wait_ge(l_p, g + 1)
                for r in range(4):
                    ins = pe.transpose(pM[0][:, r * P:(r + 1) * P],
                                       PL[:, 4 * r:4 * r + 4, :].rearrange("p h j -> p (h j)"), ident)
                ins.then_inc(l_pT, 1)

            def local_pv(g):
                pe.wait_ge(l_pTc, g + 1)
                passed(pe, g)
                for b in range(GB):
                    for r in range(4):
                        ins = pe.matmul(pM[1][32 * r:32 * r + 32, N * b:N * b + N], Vbd[:, b, 32 * r:32 * r + 32],
                                        PLT[:, r, N * b:N * b + N], start=True, stop=True)
                ins.then_inc(l_o, 1)

            def local_out(g):
                pe.wait_ge(l_oc, g + 1)
                pe.matmul(pM[1][:, P:2 * P], oT[:, :], Wout[:, :], start=True, stop=True).then_inc(l_y, 1)

            def body(it, first=False, last=False):
                for k in range(GB):
                    b = it * GB + k
                    if not (last and k >= GB - 2):
                        scores(b + 2, (k + 2) % GB, it + (k + 2) // GB)
                    if k == 0 and not first:
                        project(it - 1, b + 3)
                    if k == 1 and not first:
                        local_T(it - 1, b + 3)
                    if k == 1 and not last:
                        qk(it + 1)
                    if k == 2 and not first:
                        local_scores(it - 1)
                    if k == 3 and not first:
                        local_pT(it - 1)
                    probs_T(b, k, 0, first and k == 0)
                    probs_T(b, k, 1, first and k == 0)
                    probs_T(b, k, 2)
                    pv(b, k, 0, first and k == 0)
                    probs_T(b, k, 3)
                    for t in range(1, T):
                        pv(b, k, t)
                    if k == 3 and not first:
                        local_pv(it - 1)
                    if not (last and k > 0):
                        if k == 0 and not first:
                            pe.wait_ge(out_copied, it)
                        if k == 1 and not first:
                            pe.wait_ge(l_xTc, it)
                        ctx_T(b + 3, (k + 3) % GB)
                    if k == 1 and not first:
                        local_qkv(it - 1)
                    if k == 3 and not first:
                        local_out(it - 1)

            pe.wait_ge(ld_loc, 64)
            body(0, first=True)
            with pe.Fori(1, G - 1) as it:
                body(it)
            body(G - 1, last=True)
            project(G - 1, B)
            pe.wait_ge(out_copied, G)
            local_T(G - 1, B)
            for stage in (local_qkv, local_scores, local_pT, local_pv, local_out):
                stage(G - 1)

            pe.wait_ge(f_n, 1)
            for g in range(G):
                ins = pe.transpose(pC[:, g * P:(g + 1) * P], fn[:, g, :], ident)
            ins.then_inc(f_T, 1)
            pe.wait_ge(f_Tc, 1)
            for g in range(G):
                ins = pe.matmul(pP[0][:, g * E:(g + 1) * E], fnT[:, g * P:(g + 1) * P], Gate[:, :], start=True, stop=True)
            ins.then_inc(f_g, 1)
            pe.wait_ge(f_w, 1)
            for g in range(G):
                ins = pe.transpose(pP[1][0:E, g * P:(g + 1) * P], gw[:, g, :], ident)
            ins.then_inc(f_wT, 1)
            pe.wait_ge(f_wTc, 1)
            for g in range(G):
                ins = pe.matmul(pA[:, g * C:(g + 1) * C], gwT[:, g * P:(g + 1) * P], B2[:, :], start=True, stop=True)
            ins.then_inc(f_b, 1)

            def hidden(e, s, loads):
                pe.wait_ge(ld_e[s], loads)
                for i in range(2):
                    pe.wait_ge(e_hc, e * 2 + i + 1)
                    for v in range(2):
                        ins = pe.matmul((pS, pP)[i][v][:, :], W1s[s][:, v, i, :], fnT[:, :], start=True, stop=True)
                    ins.then_inc(e_h, 1)

            def down(e, s):
                pe.wait_ge(e_hT, e * 2 + 2)
                pe.wait_ge(e_yc, e + 1)
                for g in range(G):
                    for i in range(2):
                        ins = pe.matmul(pA[:, g * C:(g + 1) * C], hT[:, i, g * P:(g + 1) * P], W2s[s][:, i, :],
                                        start=(i == 0), stop=(i == 1))
                ins.then_inc(e_y, 1)

            with pe.Fori(0, E // EB) as it:
                for i in range(EB):
                    hidden(it * EB + i, i, it * 32 + 32)
                    if i:
                        down(it * EB + i - 1, i - 1)
                down(it * EB + EB - 1, EB - 1)

        @block.vector
        def _(dve):
            ch = Chain(dve, dve_step)
            link = ch.link

            def inv_sqrt(out, var, eps, n):
                v, i0, a = nt_v[:, 0:n], nt_i[:, 0:n], nt_a[:, 0:n]
                link(dve.tensor_scalar(v, var, eps, None, ALU.add))
                link(dve.tensor_scalar(i0, v.bitcast(I32), 1, None, ALU.logical_shift_right))
                link(dve.tensor_scalar(out.bitcast(I32), i0, -1, MAGIC, ALU.mult, ALU.add))
                for _ in range(3):
                    link(dve.tensor_tensor(a, out, out, ALU.mult))
                    link(dve.scalar_tensor_tensor(a, a, -0.5, v, ALU.mult, ALU.mult))
                    link(dve.scalar_tensor_tensor(out, a, 1.5, out, ALU.add, ALU.mult))

            def norm_rows(dst, src, eps, n):
                passed(dve, ch.base)
                for g in range(n):
                    ins = dve.bn_stats(xstat[:, g, :], src(g))
                link(ins)
                passed(dve, ch.base)
                for g in range(n):
                    ins = dve.bn_aggr(xmv[:, g, :], xstat[:, g, :])
                link(ins)
                inv_sqrt(xrs[:, 0:n], xmv[:, 0:n, 1], eps, n)
                for g in range(n):
                    ins = dve.tensor_scalar(dst(g), src(g), xmv[:, g, 0:1], xrs[:, g:g + 1], ALU.subtract, ALU.mult)
                return ins

            def place(blk, src, done):
                for e in range(2):
                    for kp in range(2):
                        start = kp * 192 + 32 * e
                        ins = dve.tensor_copy(blk[64 * e:64 * e + 64, start:start + 3 * 257 + 1:257], src(e, kp))
                ins.then_inc(done, 1)

            dve.wait_ge(ld_vec, 16)
            dve.wait_ge(blk_zero, 3)
            place(NKblk, lambda e, kp: VEC[64 * e:64 * e + 64, V_NK:V_NK + 1].broadcast_to([64, 4]), nk_placed)
            dve.wait_ge(ld_x, 16)
            link(norm_rows(lambda g: rowtmp[:, g, :], lambda g: X[:, g, :], 1e-5, G))
            norm_rows(lambda g: rowtmp[:, g, :], lambda g: rowtmp[:, g, :], 1e-6, G).then_inc(x_normed, 1)

            def ctx_stats(g, k):
                passed(dve, g)
                for t in range(T):
                    src = CTX[:, GB * g + k, t, :] if isinstance(g, int) else col(CTX, g * GB + k)[:, t, :]
                    ins = dve.bn_stats(cstat[:, k * T + t, :], src)
                return ins

            def ctx_inv(k, n):
                c = slice(k * T, (k + n) * T)
                passed(dve, ch.base)
                for i in range(k * T, (k + n) * T):
                    ins = dve.bn_aggr(cmv[:, i, :], cstat[:, i, :])
                link(ins)
                inv_sqrt(crs[:, c], cmv[:, c, 1], 1e-6, n * T)

            def ctx_apply(g, k):
                for t in range(T):
                    src = CTX[:, GB * g + k, t, :] if isinstance(g, int) else col(CTX, g * GB + k)[:, t, :]
                    n = k * T + t
                    ins = dve.tensor_scalar(NC[:, k, t, :], src, cmv[:, n, 0:1], crs[:, n:n + 1], ALU.subtract, ALU.mult)
                ins.then_inc(ctx_normed, 1)

            dve.wait_ge(xT_ready, 1)
            dve.tensor_scalar(xnT[:, :], pM[1][:, :], VEC[:, V_LN1S:V_LN1S + 1], VEC[:, V_LN1B:V_LN1B + 1],
                              ALU.mult, ALU.add).then_inc(xT_copied, 1)
            dve.wait_ge(vb_ready, 1)
            link(dve.tensor_scalar(nvk[:, :], pA[:, 0:KC], -1.0, VEC[:, V_NV:V_NV + 1], ALU.mult, ALU.add))
            place(NVblk, lambda e, kp: nvk[64 * e:64 * e + 64, kp:KC:2], nv_placed)
            dve.wait_ge(ld_ctx[0], 16)
            for k in range(GB):
                ins = ctx_stats(0, k)
            link(ins)
            ctx_inv(0, GB)
            for k in range(GB - 1):
                ctx_apply(0, k)
            dve.wait_ge(sn_copied, 1)
            link(dve.transpose(SNR[:, :, :].rearrange("p b g -> p (b g)"), sn_pad[:, :]))

            def mask_max(b, k):
                dve.wait_ge(mask_ready, b + 1)
                for q in range(HG):
                    dve.wait_ge(scores_ready, b * HG + q + 1)
                    passed(dve, b)
                    ins = dve.tensor_tensor_reduce(SM[:, k, q, :], pS[q % 2][:, :], MB[:, k % 2, :], 1.0, -BIG,
                                                   ALU.add, ALU.max, mrow[:, k, q:q + 1])
                    ins.then_inc(masked, 1)
                dve.wait_ge(masked, b * HG + HG)
                null = col(SNR, b)[:, 0:HG]
                link(dve.tensor_tensor(mx4[:, :], mrow[:, k, :], null, ALU.max))
                link(dve.tensor_scalar(negm[:, k, :], mx4[:, :], -SCALE, None, ALU.mult))
                dve.scalar_tensor_tensor(snm[:, k, :], null, SCALE, negm[:, k, :], ALU.mult,
                                         ALU.add).then_inc(shift_ready, 1)

            def sums(b, k):
                dve.wait_ge(exp_done, (b + 1) * (HG + 1))
                link(dve.tensor_tensor(lsum[:, :], rsum[:, k, :], pn[:, k, :], ALU.add))
                link(dve.reciprocal(rinv[:, k, :], lsum[:, :]))
                for q in range(HG):
                    dve.tensor_scalar(SM[:, k, q, :], SM[:, k, q, :], rinv[:, k, q:q + 1], None,
                                      ALU.mult).then_inc(probs_normed, 1)
                link(dve.tensor_tensor(PNR[:, k, 0:HG], pn[:, k, :], rinv[:, k, :], ALU.mult))

            def local_norm(g):
                xr = col(X, g)
                dve.wait_ge(out_copied, g + 1)
                link(norm_rows(lambda _: y1[:, :], lambda _: OUT1[:, :], 1e-6, 1))
                link(dve.tensor_tensor(y1[:, :], y1[:, :], ROWS[:, 0, :], ALU.mult))
                link(dve.tensor_tensor(y1[:, :], y1[:, :], ROWS[:, 1, :], ALU.add))
                link(dve.tensor_tensor(xr, xr, y1[:, :], ALU.add))
                norm_rows(lambda _: xg[:, :], lambda _: xr, 1e-5, 1).then_inc(l_xn, 1)

            def local_qkv(g):
                dve.wait_ge(l_k, g + 1)
                dve.tensor_scalar(qT[:, :], pM[0][:, 0:P], VEC[:, V_BQ:V_BQ + 1], LD ** -0.5, ALU.add, ALU.mult)
                link(dve.tensor_scalar(kTe[:, :, 0:N], pM[0][:, P:2 * P].rearrange("p (b i) -> p b i", b=GB),
                                       VEC[:, V_BK:V_BK + 1], None, ALU.add))
                for r in range(LR):
                    ins = dve.tensor_scalar(Kbd[:, :, r, :], kTe[:, :, :], CON[:, K_R + r:K_R + r + 1], None, ALU.mult)
                ins.then_inc(l_kc, 1)
                dve.wait_ge(l_v, g + 1)
                dve.tensor_tensor(Vbd[:, :, :], pM[1][:, :].rearrange("p (b c) -> p b c", b=GB),
                                  CON[:, K_V:K_V + C].unsqueeze(1).broadcast_to([P, GB, C]), ALU.mult).then_inc(l_vc, 1)

            def local_max(g):
                dve.wait_ge(l_s1, g * 2 + 2)
                views = [pM[i][:, 0:2 * LR * LJ].rearrange("p (h j) -> p h j", j=LJ) for i in range(2)]
                for i in range(2):
                    ins = dve.tensor_reduce(lmax[:, 8 * i:8 * i + 8], views[i], AX.X, ALU.max)
                link(ins)
                for i in range(2):
                    ins = dve.tensor_tensor(SL[:, 8 * i:8 * i + 8, :], views[i],
                                            lmax[:, 8 * i:8 * i + 8].unsqueeze(2).broadcast_to([P, 8, LJ]),
                                            ALU.subtract)
                ins.then_inc(l_sub, 1)

            def local_probs(g):
                dve.wait_ge(l_exp, g + 1)
                link(dve.tensor_scalar(SL[:, :, N:LJ], SL[:, :, N:LJ], float(PADS), None, ALU.mult))
                link(dve.tensor_reduce(lden[:, :], SL[:, :, :], AX.X, ALU.add))
                link(dve.reciprocal(lrec[:, :], lden[:, :]))
                dve.tensor_tensor(PL[:, :, :], SL[:, :, 0:N], lrec[:, :].unsqueeze(2).broadcast_to([P, 16, N]),
                                  ALU.mult).then_inc(l_p, 1)

            def local_o(g):
                dve.wait_ge(l_o, g + 1)
                dve.tensor_scalar(oT[:, :], pM[1][:, 0:P], VEC[:, V_BV:V_BV + 1], None, ALU.add).then_inc(l_oc, 1)

            def local_add(g):
                xr = col(X, g)
                dve.wait_ge(l_y, g + 1)
                link(dve.tensor_tensor(xr, xr, pM[1][:, P:2 * P], ALU.add))
                link(dve.tensor_tensor(xr, xr, ROWS[:, 2, :], ALU.add))

            mask_max(0, 0)
            mask_max(1, 1)
            sums(0, 0)
            for g in range(1, G):
                dve.wait_ge(ld_ctx[g], 16)
            dve.wait_ge(ld_rows, 16)
            for b in range(GB):
                ins = dve.tensor_copy(kTe[:, b, N:LJ], VEC[:, V_BK:V_BK + 1])
            link(ins)

            def body(it, first=False, last=False):
                for k in range(GB):
                    b = it * GB + k
                    if k == 2 and not first:
                        local_qkv(it - 1)
                    if k == 3 and not first:
                        local_probs(it - 1)
                    if not (last and k >= GB - 2):
                        mask_max(b + 2, (k + 2) % GB)
                    if k == GB - 1:
                        if not first:
                            dve.wait_ge(out_ready, it)
                        dve.transpose(PNT[:, :], PNR[:, :, :].rearrange("p k g -> p (k g)")).then_inc(pnT_ready, 1)
                        dve.wait_ge(pnT_ready, it + 1)
                    if not (last and k == GB - 1):
                        sums(b + 1, (k + 1) % GB)
                    if not last and k in (1, 2):
                        n = 2 * (k - 1)
                        ctx_stats(it + 1, n)
                        link(ctx_stats(it + 1, n + 1))
                        ctx_inv(n, 2)
                    if not (last and k > 0):
                        if not (first and k == 0):
                            dve.wait_ge(pv_ready, b)
                        ctx_apply(it + (k + 3) // GB, (k + 3) % GB)
                    if k == 0 and not first:
                        local_norm(it - 1)
                    if k == 2 and not first:
                        local_max(it - 1)
                    if k == 3 and not first:
                        local_o(it - 1)
                        local_add(it - 1)

            body(0, first=True)
            with dve.Fori(1, G - 1) as it:
                ch.loop(it - 1, BODY_STEPS)
                body(it)
            ch.end(G - 2)
            body(G - 1, last=True)
            for stage in (local_norm, local_qkv, local_max, local_probs, local_o, local_add):
                stage(G - 1)

            norm_rows(lambda g: fn[:, g, :], lambda g: X[:, g, :], 1e-5, G).then_inc(f_n, 1)
            dve.tensor_scalar(b1v[:, :, :], VEC[:, V_B1:V_B1 + 4 * E].rearrange("p (e v i) -> p e v i", v=2, i=2)[:, :, 1, :],
                              1.0, None, ALU.add)
            dve.wait_ge(f_g, 1)
            link(dve.tensor_copy(gt[:, :, :].rearrange("p g e -> p (g e)"), pP[0][:, 0:G * E]))

            def bc(t):
                return t[:, :].unsqueeze(2).broadcast_to([P, G, E])

            def first_best(src, m, one_hot):
                link(dve.tensor_reduce(m[:, :], src[:, :, :], AX.X, ALU.max))
                link(dve.tensor_tensor(g_a[:, :, :], src[:, :, :], bc(m), ALU.is_equal))
                link(dve.tensor_tensor(g_a[:, :, :], g_a[:, :, :],
                                       CON[:, K_IOTA:K_IOTA + E].unsqueeze(1).broadcast_to([P, G, E]), ALU.mult))
                link(dve.tensor_reduce(gi[:, :], g_a[:, :, :], AX.X, ALU.max))
                link(dve.tensor_tensor(one_hot[:, :, :], g_a[:, :, :], bc(gi), ALU.is_equal))

            first_best(gt, gm1, g_is1)
            link(dve.scalar_tensor_tensor(g_rest[:, :, :], g_is1[:, :, :], -BIG, gt[:, :, :], ALU.mult, ALU.add))
            first_best(g_rest, gm2, g_is2)
            dve.tensor_tensor(gd[:, :], gm2[:, :], gm1[:, :], ALU.subtract).then_inc(f_gd, 1)
            dve.wait_ge(f_ge, 1)
            link(dve.tensor_scalar(gp1[:, :], gp2[:, :], 1.0, None, ALU.add))
            link(dve.reciprocal(gp1[:, :], gp1[:, :]))
            link(dve.tensor_tensor(gp2[:, :], gp2[:, :], gp1[:, :], ALU.mult))
            link(dve.tensor_tensor(g_is1[:, :, :], g_is1[:, :, :], bc(gp1), ALU.mult))
            link(dve.tensor_tensor(g_is2[:, :, :], g_is2[:, :, :], bc(gp2), ALU.mult))
            link(dve.tensor_tensor(gw[:, :, :], g_is1[:, :, :], g_is2[:, :, :], ALU.add))
            dve.sem_inc(f_w, 1)
            dve.wait_ge(f_b, 1)
            dve.tensor_tensor(X[:, :, :].rearrange("p g c -> p (g c)"), X[:, :, :].rearrange("p g c -> p (g c)"),
                              pA[:, :], ALU.add).then_inc(e_yc, 1)

            def clip(e):
                for i in range(2):
                    dve.wait_ge(e_h, e * 2 + i + 1)
                    bias = VEC[:, bass.ds(e * 4 + V_B1 + i, 1)]
                    dve.tensor_scalar(hg[:, i, :], (pS, pP)[i][0][:, :], bias, 9.0, ALU.add, ALU.min)
                    dve.tensor_scalar(hv[:, i, :], (pS, pP)[i][1][:, :], col(b1v, e)[:, i:i + 1], -8.0, ALU.add,
                                      ALU.max).then_inc(e_hc, 1)

            def swiglu(e, first=False):
                for i in range(2):
                    dve.wait_ge(e_sg, e * 2 + i + 1)
                    if i == 0 and not first:
                        dve.wait_ge(e_y, e)
                    dve.scalar_tensor_tensor(hT[:, i, :], hv[:, i, :], 10.0, hs[:, i, :], ALU.min,
                                             ALU.mult).then_inc(e_hT, 1)

            def add_expert(e):
                dve.wait_ge(e_y, e + 1)
                dve.wait_ge(e_yc, e + 1)
                for g in range(G):
                    ins = dve.scalar_tensor_tensor(X[:, g, :], pA[:, g * C:(g + 1) * C], gw[:, g, bass.ds(e, 1)],
                                                   X[:, g, :], ALU.mult, ALU.add)
                ins.then_inc(e_yc, 1)

            dve.sem_inc(e_hc, 2)
            clip(0)
            dve.wait_ge(e_hc, 4)
            swiglu(0, True)
            with dve.Fori(0, E - 1) as e:
                dve.wait_ge(e_hT, e * 2 + 2)
                clip(e + 1)
                add_expert(e)
                dve.wait_ge(e_hc, e * 2 + 6)
                swiglu(e + 1)
            add_expert(E - 1)


def kernel(**inputs):
    import numpy as np
    import concourse.bacc as bacc
    from concourse.bass_utils import run_bass_kernel_spmd as run

    a = {n: np.asarray(v) for n, v in inputs.items()}
    wq, wkv, wo = a["L0_xattn_Wq"], a["L0_xattn_Wkv"], a["L0_xattn_Wo"]
    nk, nv = a["L0_xattn_null_kv"]
    bqkv = a["L0_attn_b_qkv"].reshape(3, C)
    b1 = a["L0_ffn_dense_1_b"].reshape(E, 2, P, 2).transpose(2, 0, 3, 1).reshape(P, 4 * E)
    vec = np.concatenate([np.stack([a["L0_xattn_ln1_s"], a["L0_xattn_ln1_b"], a["L0_xattn_lnc_s"], a["L0_xattn_lnc_b"],
                                    bqkv[0], bqkv[1], bqkv[2], np.concatenate([nk, nk]), np.concatenate([nv, nv])],
                                   axis=1), b1], axis=1)
    rows = np.stack([a["L0_xattn_lno_s"], a["L0_xattn_lno_b"], a["L0_attn_b_out"]])[None]
    ch = np.arange(P)
    const = np.zeros((P, K_COLS), np.float32)
    const[:, K_ID:K_ID + P] = np.eye(P)
    const[:, K_R:K_R + LR] = (ch[:, None] // LD) % LR == np.arange(LR)[None]
    const[:, K_V:K_V + C] = ch[:, None] // N == (ch[None] // LD) % LR
    const[:, K_IOTA:K_IOTA + E] = E - np.arange(E)
    w1 = a["L0_ffn_dense_1_w"].reshape(E, 2, P, 2, C).transpose(0, 4, 3, 1, 2)
    w2 = a["L0_ffn_dense_2_w"].reshape(E, C, 2, P).transpose(0, 3, 2, 1)
    mask = a["mask_BxS2_bf1"].view(np.uint8).reshape(B, P, T).transpose(0, 2, 1).reshape(1, B * M)
    arrays = {
        "x": a["x"].reshape(B * N, C), "ctx_in": a["ctx_1024"].reshape(B * M, C), "mask": mask, "vec": vec,
        "rows": rows, "const": const, "wqT": wq.T, "wkT": wkv[:, :H * D].T, "wvT": wkv[:, H * D:].T,
        "wv": wkv[:, H * D:], "wo": wo, "wqkv": a["L0_attn_w_qkv"], "wout": a["L0_attn_w_out"],
        "gate": a["L0_ffn_gate_w"], "w1": w1, "w2": w2, "b2": a["L0_ffn_dense_2_b"],
    }
    arrays = {f"{n}_dram": np.ascontiguousarray(v) for n, v in arrays.items()}
    nc = bacc.Bacc("TRN2", target_bir_lowering=False, num_devices=1)
    aps = [nc.dram_tensor(n, v.shape, mybir.dt.from_np(v.dtype), kind="ExternalInput").ap() for n, v in arrays.items()]
    out = nc.dram_tensor("out_dram", (B * N, C), F32, kind="ExternalOutput").ap()
    perceiver(nc, *aps, out)
    result = run(nc, [arrays], core_ids=[0])
    return result.results[0]["out_dram"].reshape(B, N, C)
```

```python
from contextlib import ExitStack
from math import exp

import concourse.bass as bass
from concourse import mybir

ALU = mybir.AluOpType
ACT = mybir.ActivationFunctionType
AX = mybir.AxisListType
F32 = mybir.dt.float32
I32 = mybir.dt.int32
BF16 = mybir.dt.bfloat16
U8 = mybir.dt.uint8

P = 128
B, N, C = 16, 32, 128
M = 512
H, D = 16, 64
GB = P // N
G = B // GB
T = M // P
HG = H // GB
KC = H * D // P
LD = C // 16
LR = 32 // LD
LJ = N + 1
PADS = 64 - N
E = 8
EB = 4
PASS = ((range(0, G - 1), slice(0, (G - 1) * P)), (range(G - 1, G), slice((G - 1) * P, G * P)))
BODY_STEPS = 54
POOL_STEPS = 33
SCALE = H ** -0.5
ALPHA, LIMIT = 1.702, 9.0
TOP = LIMIT / (1 + exp(-ALPHA * LIMIT))
BIG = 3e38
MAGIC = 0x5F3759DF

V_LN1S, V_LN1B, V_LNCS, V_LNCB, V_BQ, V_BK, V_BV, V_NK, V_NV = range(9)
V_B1 = 9
V_N = V_B1 + E * 4
K_ID, K_R, K_V, K_IOTA = 0, P, P + LR, 2 * P + LR
K_COLS = K_IOTA + E


def col(t, i):
    return t[:, i] if isinstance(i, int) else t[:, bass.ds(i, 1)].squeeze(1)


class Chain:

    def __init__(self, eng, sem):
        self.eng, self.sem, self.n, self.base = eng, sem, 0, 0

    def link(self, ins):
        ins.then_inc(self.sem, 1)
        self.n += 1
        self.eng.wait_ge(self.sem, self.base + self.n)

    def loop(self, it, per_body):
        self.start = self.n
        self.base = it * per_body
        self.per_body = per_body

    def end(self, times):
        assert self.n - self.start == self.per_body, (self.n - self.start, self.per_body)
        self.n += (times - 1) * self.per_body
        self.base = 0


def inv_sqrt(eng, link, tmp, out, var, eps, n, stt):
    v, a = (t[:, 0:n] for t in tmp)
    link(eng.tensor_scalar(v, var, eps, None, ALU.add))
    link(eng.tensor_scalar(out.bitcast(I32), v.bitcast(I32), -0.5, float(MAGIC), ALU.mult, ALU.add))
    for _ in range(3):
        link(eng.tensor_tensor(a, out, out, ALU.mult))
        if stt:
            link(eng.scalar_tensor_tensor(a, a, -0.5, v, ALU.mult, ALU.mult))
            link(eng.scalar_tensor_tensor(out, a, 1.5, out, ALU.add, ALU.mult))
        else:
            link(eng.tensor_tensor(a, a, v, ALU.mult))
            link(eng.tensor_scalar(a, a, -0.5, 1.5, ALU.mult, ALU.add))
            link(eng.tensor_tensor(out, out, a, ALU.mult))


def perceiver(nc, x, ctx_in, mask, vec, rows, const, wqT, wkT, wvT, wv, wo, wqkv, wout, gate, w1, w2, b2, out):
    with ExitStack() as ctx:
        def sb(name, shape, dt=F32):
            return ctx.enter_context(nc.sbuf_tensor(name, shape, dt))

        def ps(name, shape=(P, 512)):
            return ctx.enter_context(nc.psum_tensor(name, list(shape), F32))

        def sem(name):
            return ctx.enter_context(nc.semaphore(name))

        X = sb("X", [P, G, C])
        VEC = sb("VEC", [P, V_N])
        ROWS = sb("ROWS", [P, 3, C])
        CON = sb("CON", [P, K_COLS])
        WqT = sb("WqT", [P, KC, C])
        WkT = sb("WkT", [P, KC, C])
        WvT = sb("WvT", [P, KC, C])
        Wv = sb("Wv", [P, H * D])
        Wo = sb("Wo", [P, KC, C])
        Wqkv = sb("Wqkv", [P, 3 * C])
        Wout = sb("Wout", [P, C])
        Gate = sb("Gate", [P, E])
        B2 = sb("B2", [E, C])
        CTX = sb("CTX", [P, B, T, C])
        MK8 = sb("MK8", [P, B, M], U8)
        MB = sb("MB", [P, 2, M], BF16)
        A = sb("A", [P, H, C])
        Bm = sb("Bm", [P, H, C])
        U = sb("U", [P, P])
        NVW = sb("NVW", [P, C])
        NKblk = sb("NKblk", [P, KC * P])
        NVblk = sb("NVblk", [P, KC * P])
        nvk = sb("nvk", [P, KC])
        xnT = sb("xnT", [P, G * P])
        sn_pad = sb("sn_pad", [P, G * P])
        SNR = sb("SNR", [P, B, N])
        rowtmp = sb("rowtmp", [P, G, C])

        NC = sb("NC", [P, GB, T, C])
        cnT = sb("cnT", [P, 2, M])
        QK = sb("QK", [P, GB, H, N])
        SM = sb("SM", [P, GB, HG, M])
        PT = sb("PT", [P, T, M])
        AC = sb("AC", [P, H, P])
        PNR = sb("PNR", [P, GB, N])
        PNT = sb("PNT", [P, P])
        OUT1 = sb("OUT1", [P, C])
        cstat = sb("cstat", [P, GB * T, 6])
        cmv = sb("cmv", [P, GB * T, 2])
        crs = sb("crs", [P, GB * T])
        cnm = sb("cnm", [P, GB * T])
        mrow = sb("mrow", [P, GB, HG])
        mx4 = sb("mx4", [P, HG])
        negm = sb("negm", [P, GB, HG])
        snm = sb("snm", [P, GB, HG])
        rsum = sb("rsum", [P, GB, HG])
        pn = sb("pn", [P, GB, HG])
        lsum = sb("lsum", [P, HG])
        rinv = sb("rinv", [P, GB, HG])
        xstat = sb("xstat", [P, G, 6])
        xmv = sb("xmv", [P, G, 2])
        xrs = sb("xrs", [P, G])
        nt_v = sb("nt_v", [P, GB * T])
        nt_a = sb("nt_a", [P, GB * T])
        cn_v = sb("cn_v", [P, 2 * T])
        cn_a = sb("cn_a", [P, 2 * T])

        y1 = sb("y1", [P, C])
        ostat = sb("ostat", [P, 6])
        omv = sb("omv", [P, 2])
        ors = sb("ors", [P, 1])
        xg = sb("xg", [P, C])
        xgT = sb("xgT", [P, P])
        XR = sb("XR", [P, GB, LR, N])
        qT = sb("qT", [P, P])
        qbias = sb("qbias", [P, 1])
        kbias = sb("kbias", [P, LR])
        Kbd = sb("Kbd", [P, GB, LR, LJ])
        Vbd = sb("Vbd", [P, GB, C])
        SL = sb("SL", [P, 16, LJ])
        PL = sb("PL", [P, 16, N])
        PLT = sb("PLT", [P, 4, P])
        lmax = sb("lmax", [P, 16])
        lden = sb("lden", [P, 16])
        lrec = sb("lrec", [P, 16])
        oT = sb("oT", [P, P])

        fn = sb("fn", [P, G, C])
        fnT = sb("fnT", [P, G * P])
        gt = sb("gt", [P, G, E])
        g_is1 = sb("g_is1", [P, G, E])
        g_a = sb("g_a", [P, G, E])
        g_rest = sb("g_rest", [P, G, E])
        g_is2 = sb("g_is2", [P, G, E])
        gw = sb("gw", [P, G, E])
        gm1 = sb("gm1", [P, G])
        gm2 = sb("gm2", [P, G])
        gi = sb("gi", [P, G])
        gd = sb("gd", [P, G])
        gp1 = sb("gp1", [P, G])
        gp2 = sb("gp2", [P, G])
        gwT = sb("gwT", [E, G * P])
        b1g = sb("b1g", [P, E, 2])
        b1v = sb("b1v", [P, E, 2])
        W1s = [sb(f"W1s{i}", [P, 2, 2, P]) for i in range(EB)]
        W2s = [sb(f"W2s{i}", [P, 2, C]) for i in range(EB)]
        for b in range(0, 2 * (E - EB), 2):
            W1s.append(CTX[:, b, :, :].rearrange("p (v i) m -> p v i m", v=2))
            W2s.append(CTX[:, b + 1, 0:2, :])
        hs, hv, hT = ([SM[:, 2 * i + j // 2, j % 2 * 2:j % 2 * 2 + 2, :] for i in range(2)] for j in range(3))

        pS = [ps("pS0"), ps("pS1")]
        pP = [ps("pP0"), ps("pP1")]
        pA, pC = ps("pA"), ps("pC")
        pM = [ps("pM0"), ps("pM1")]

        ld_x, ld_vec, ld_con, ld_rows = sem("ld_x"), sem("ld_vec"), sem("ld_con"), sem("ld_rows")
        ld_wq, ld_wk, ld_wvT, ld_wv, ld_wo = sem("ld_wq"), sem("ld_wk"), sem("ld_wvT"), sem("ld_wv"), sem("ld_wo")
        ld_ctx = [sem(f"ld_ctx{g}") for g in range(G)]
        ld_mask = sem("ld_mask")
        ld_loc = sem("ld_loc")
        ld_e = [sem(f"ld_e{e}") for e in range(E)]
        dve_step, pool_step = sem("dve_step"), sem("pool_step")
        tile_normed = sem("tile_normed")
        moments_ready = sem("moments_ready")
        out_inv = sem("out_inv")
        inv_ready = sem("inv_ready")
        mask_copied = sem("mask_copied")
        mask_ready = sem("mask_ready")
        wait_passed = {e.engine: sem(f"wait_passed_{n}") for n, e in
                       (("dve", nc.vector), ("pe", nc.tensor), ("pool", nc.gpsimd))}
        blk_zero = sem("blk_zero")
        x_normed, xT_ready, xT_copied = sem("x_normed"), sem("xT_ready"), sem("xT_copied")
        nk_placed, u_ready, u_copied = sem("nk_placed"), sem("u_ready"), sem("u_copied")
        vb_ready, nv_placed = sem("vb_ready"), sem("nv_placed")
        nvw_ready, nvw_copied = sem("nvw_ready"), sem("nvw_copied")
        wA_ready, wA_copied = sem("wA_ready"), sem("wA_copied")
        wB_ready, wB_copied = sem("wB_ready"), sem("wB_copied")
        masked = sem("masked")
        sn_ready, sn_copied = sem("sn_ready"), sem("sn_copied")
        ctx_normed, cT_ready, cT_copied = sem("ctx_normed"), sem("cT_ready"), sem("cT_copied")
        qk_ready, qk_copied = sem("qk_ready"), sem("qk_copied")
        scores_ready, shift_ready, exp_done = sem("scores_ready"), sem("shift_ready"), sem("exp_done")
        probs_normed = sem("probs_normed")
        probsT_ready, pt_copied = sem("probsT_ready"), sem("pt_copied")
        pv_ready, ac_copied, pnT_ready = sem("pv_ready"), sem("ac_copied"), sem("pnT_ready")
        out_ready, out_copied = sem("out_ready"), sem("out_copied")
        local_normed, local_xT_ready, local_xT_copied = sem("local_normed"), sem("local_xT_ready"), sem("local_xT_copied")
        local_keys_ready, local_values_ready = sem("local_keys_ready"), sem("local_values_ready")
        local_keys_placed, local_values_placed = sem("local_keys_placed"), sem("local_values_placed")
        biases_ready = sem("biases_ready")
        local_scores_ready, local_shifted = sem("local_scores_ready"), sem("local_shifted")
        local_exp_done, local_probs_ready = sem("local_exp_done"), sem("local_probs_ready")
        local_probsT_ready, local_probsT_copied = sem("local_probsT_ready"), sem("local_probsT_copied")
        local_oT_ready, local_oT_copied, local_y_ready = sem("local_oT_ready"), sem("local_oT_copied"), sem("local_y_ready")
        ffn_normed, ffn_xT_ready, ffn_xT_copied = sem("ffn_normed"), sem("ffn_xT_ready"), sem("ffn_xT_copied")
        gate_ready, gate_copied = sem("gate_ready"), sem("gate_copied")
        gate_diff_ready, gate_exp_done = sem("gate_diff_ready"), sem("gate_exp_done")
        weights_ready, weightsT_ready, weightsT_copied = sem("weights_ready"), sem("weightsT_ready"), sem("weightsT_copied")
        bias_sum_ready = sem("bias_sum_ready")
        hidden_ready = sem("hidden_ready")
        activated = sem("activated")
        clipped = sem("clipped")
        hT_ready = sem("hT_ready")
        down_ready = sem("down_ready")
        expert_added = sem("expert_added")
        out_done = sem("out_done")
        x1_ready, st_out = sem("x1_ready"), sem("st_out")

        def passed(eng, i):
            if not isinstance(i, int):
                eng.sem_inc(wait_passed[eng.engine], 1)

        ident = CON[:, K_ID:K_ID + P]
        block = ctx.enter_context(nc.Block())

        @block.sync
        def _(sp):
            sp.dma_start(X[:, :, :], x.rearrange("(g p) c -> p g c", p=P)).then_inc(ld_x, 16)
            sp.dma_start(VEC[:, :], vec).then_inc(ld_vec, 16)
            sp.dma_start(CON[:, :], const).then_inc(ld_con, 16)
            for g in range(G):
                sp.dma_start(CTX[:, GB * g:GB * (g + 1), :, :],
                             ctx_in[GB * g * M:GB * (g + 1) * M, :].rearrange("(b p t) c -> p b t c", p=P, t=T)
                             ).then_inc(ld_ctx[g], 16)
                if g == 0:
                    sp.dma_start(Wv[:, :], wv).then_inc(ld_wv, 16)
            sp.dma_start(ROWS[:, :, :], rows.broadcast_to([P, 3, C])).then_inc(ld_rows, 16)
            sp.dma_start(Wqkv[:, :], wqkv).then_inc(ld_loc, 16)
            sp.dma_start(Wout[:, :], wout).then_inc(ld_loc, 16)
            sp.dma_start(Gate[:, :], gate).then_inc(ld_loc, 16)
            sp.dma_start(B2[:, :], b2).then_inc(ld_loc, 16)
            for e in range(E):
                if e == EB:
                    sp.wait_ge(ctx_normed, 2 * GB)
                    sp.wait_ge(tile_normed, GB)
                sp.dma_start(W1s[e][:, :, :, :], w1[e]).then_inc(ld_e[e], 16)
                sp.dma_start(W2s[e][:, :, :], w2[e]).then_inc(ld_e[e], 16)
            most = G - 1
            sp.wait_ge(out_done, 1)
            sp.dma_start(out[0:most * P, :].rearrange("(g p) c -> p g c", p=P), X[:, 0:most, :]).then_inc(st_out, 16)
            sp.wait_ge(out_done, 2)
            sp.dma_start(out[most * P:G * P, :], X[:, most, :]).then_inc(st_out, 16)
            sp.wait_ge(st_out, 32)

        @block.gpsimd
        def _(pool):
            pool.memset(NKblk[:, :], 0.0).then_inc(blk_zero, 1)
            pool.memset(NVblk[:, :], 0.0).then_inc(blk_zero, 1)
            pool.memset(PNR[:, :, :], 0.0).then_inc(blk_zero, 1)

            def mask_bias(b, k):
                pool.tensor_copy(MB[:, k, :], col(MK8, b)).then_inc(mask_copied, 1)
                pool.wait_ge(mask_copied, b + 1)
                passed(pool, b)
                pool.tensor_scalar(MB[:, k, :], MB[:, k, :], BIG, -BIG, ALU.mult, ALU.add).then_inc(mask_ready, 1)

            ch = Chain(pool, pool_step)

            def link(ins):
                ch.link(ins)
                passed(pool, ch.base)

            def ctx_inv(k, pairs):
                c = slice(k * T, (k + 2) * T)
                pool.wait_ge(moments_ready, pairs)
                passed(pool, pairs)
                inv_sqrt(pool, link, (cn_v, cn_a), crs[:, c], cmv[:, c, 1], 1e-6, 2 * T, False)
                link(pool.tensor_tensor(cnm[:, c], cmv[:, c, 0], crs[:, c], ALU.mult))
                pool.tensor_scalar(cnm[:, c], cnm[:, c], -1.0, None, ALU.mult).then_inc(inv_ready, 1)

            def out_norm(g):
                xr = col(X, g)
                pool.wait_ge(out_inv, g + 1)
                passed(pool, g)
                link(pool.tensor_scalar(y1[:, :], OUT1[:, :], omv[:, 0:1], ors[:, :], ALU.subtract, ALU.mult))
                link(pool.tensor_tensor(y1[:, :], y1[:, :], ROWS[:, 0, :], ALU.mult))
                link(pool.tensor_tensor(y1[:, :], y1[:, :], ROWS[:, 1, :], ALU.add))
                pool.tensor_tensor(xr, xr, y1[:, :], ALU.add).then_inc(x1_ready, 1)

            pool.wait_ge(ld_mask, 16)
            mask_bias(0, 0)
            mask_bias(1, 1)
            ctx_inv(2, 1)

            def masks(b):
                for k in range(2):
                    pool.wait_ge(masked, (b + k - 1) * HG)
                    mask_bias(b + k, k)

            def body(it, first=False):
                masks(it * GB + 2)
                ctx_inv(0, it * 2 + 2)
                if not first:
                    out_norm(it - 1)
                masks(it * GB + 4)
                ctx_inv(2, it * 2 + 3)

            body(0, first=True)
            pool.wait_ge(ld_rows, 16)
            with pool.Fori(1, G - 1) as it:
                ch.loop(it - 1, POOL_STEPS)
                body(it)
            ch.end(G - 2)
            masks((G - 1) * GB + 2)
            out_norm(G - 2)
            out_norm(G - 1)

        @block.scalar
        def _(act):
            act.dma_start(WqT[:, :, :], wqT.rearrange("(k p) c -> p k c", p=P)).then_inc(ld_wq, 16)
            act.dma_start(WkT[:, :, :], wkT.rearrange("(k p) c -> p k c", p=P)).then_inc(ld_wk, 16)
            act.dma_start(WvT[:, :, :], wvT.rearrange("(k p) c -> p k c", p=P)).then_inc(ld_wvT, 16)
            act.dma_start(Wo[:, :, :], wo.rearrange("(k p) c -> p k c", p=P)).then_inc(ld_wo, 16)
            act.dma_start(MK8[:, :, :].rearrange("p b m -> p (b m)"), mask.broadcast_to([P, B * M])).then_inc(ld_mask, 16)

            def copy_cT(b, k, first=False):
                act.wait_ge(cT_ready, b + 1)
                if not first:
                    act.wait_ge(scores_ready, b * HG - HG)
                act.activation(cnT[:, k % 2, :], pC[:, :], ACT.Identity, bias=VEC[:, V_LNCB:V_LNCB + 1],
                               scale=VEC[:, V_LNCS:V_LNCS + 1]).then_inc(cT_copied, 1)

            def copy_qk(g, first=False):
                for q in range(HG):
                    act.wait_ge(qk_ready, g * HG + q + 1)
                    if q == 0 and not first:
                        act.wait_ge(scores_ready, g * GB * HG)
                    act.copy(QK[:, :, GB * q:GB * (q + 1), :].rearrange("p k h i -> p h k i"),
                             pM[q % 2][:, :].rearrange("p (h k i) -> p h k i", h=GB, k=GB)).then_inc(qk_copied, 1)

            def exps(b, k, quartets=range(HG)):
                if 0 in quartets:
                    act.wait_ge(shift_ready, b + 1)
                    act.activation(pn[:, k, :], snm[:, k, :], ACT.Exp).then_inc(exp_done, 1)
                for q in quartets:
                    act.activation(SM[:, k, q, :], SM[:, k, q, :], ACT.Exp, bias=negm[:, k, q:q + 1],
                                   scale=SCALE, accum_out=rsum[:, k, q:q + 1]).then_inc(exp_done, 1)

            def copy_pT(b, tiles, first=False):
                for t in tiles:
                    act.wait_ge(probsT_ready, b * T + t + 1)
                    if t == 0 and not first:
                        act.wait_ge(pv_ready, b)
                    act.copy(PT[:, t, :], pP[t % 2][:, :]).then_inc(pt_copied, 1)

            def ctx_apply(g, k):
                if k % 2 == 0:
                    act.wait_ge(inv_ready, g * 2 + k // 2)
                for t in range(T - 1):
                    n = k * T + t
                    ins = act.activation(NC[:, k, t, :], col(CTX, g * GB + k)[:, t, :],
                                         ACT.Identity, bias=cnm[:, n:n + 1], scale=crs[:, n:n + 1])
                ins.then_inc(ctx_normed, 1)

            def copy_ac(b, k, reads=None):
                act.wait_ge(pv_ready, b + 1)
                if reads is not None:
                    act.wait_ge(out_ready, reads)
                act.activation(AC[:, :, N * k:N * k + N], pA[:, :].rearrange("p (h i) -> p h i", h=H), ACT.Identity,
                               bias=VEC[:, V_LNCB:V_LNCB + 1], scale=VEC[:, V_LNCS:V_LNCS + 1]).then_inc(ac_copied, 1)

            def copy_out(g):
                act.wait_ge(out_ready, g + 1)
                act.copy(OUT1[:, :], pC[:, 0:C]).then_inc(out_copied, 1)

            def copy_xgT(g):
                act.wait_ge(local_xT_ready, g + 1)
                act.copy(xgT[:, :], pC[:, 0:P])
                act.copy(XR[:, :, :, :], pC[:, 0:P].rearrange("p (b i) -> p b i", b=GB).unsqueeze(2)
                         .broadcast_to([P, GB, LR, N])).then_inc(local_xT_copied, 1)

            def local_qk(g):
                act.wait_ge(local_keys_ready, g + 1)
                act.activation(qT[:, :], pM[0][:, 0:P], ACT.Identity, bias=qbias[:, :], scale=LD ** -0.5)
                for r in range(LR):
                    ins = act.activation(Kbd[:, :, r, 0:N], pM[0][:, P:2 * P].rearrange("p (b i) -> p b i", b=GB),
                                         ACT.Identity, bias=kbias[:, r:r + 1], scale=CON[:, K_R + r:K_R + r + 1])
                ins.then_inc(local_keys_placed, 1)

            def local_exp(g):
                act.wait_ge(local_shifted, g + 1)
                act.activation(SL[:, :, :], SL[:, :, :], ACT.Exp).then_inc(local_exp_done, 1)

            def copy_plT(g):
                act.wait_ge(local_probsT_ready, g + 1)
                act.copy(PLT[:, :, :].rearrange("p a b -> p (a b)"), pM[0][:, :]).then_inc(local_probsT_copied, 1)

            def copy_heads(W, banks, q, done):
                for e in range(2):
                    ins = act.copy(W[:, 4 * q + e:4 * q + 4:2, :],
                                   banks[q % 2][e][:, 0:2 * C].rearrange("p (a c) -> p a c", a=2))
                ins.then_inc(done, 1)

            act.wait_ge(u_ready, 1)
            act.copy(U[:, :], pC[:, 0:P]).then_inc(u_copied, 1)
            for q in range(H // 4):
                act.wait_ge(wA_ready, q + 1)
                copy_heads(A, (pP, pS), q, wA_copied)

            def copy_Bm(q):
                act.wait_ge(wB_ready, q + 1)
                copy_heads(Bm, (pP, pM), q, wB_copied)

            copy_Bm(0)
            copy_Bm(1)
            act.wait_ge(xT_ready, 1)
            act.activation(xnT[:, :], pS[1][:, :], ACT.Identity, bias=VEC[:, V_LN1B:V_LN1B + 1],
                           scale=VEC[:, V_LN1S:V_LN1S + 1]).then_inc(xT_copied, 1)
            act.wait_ge(sn_ready, 1)
            act.copy(sn_pad[:, :], pS[0][:, :]).then_inc(sn_copied, 1)
            copy_qk(0, True)
            copy_cT(0, 0, True)
            copy_Bm(2)
            copy_cT(1, 1, True)
            copy_Bm(3)
            exps(0, 0)
            act.wait_ge(nvw_ready, 1)
            act.copy(NVW[:, :], pA[:, 0:C]).then_inc(nvw_copied, 1)
            copy_cT(2, 2)

            def body(it, first=False, last=False):
                for k in range(GB):
                    b = it * GB + k
                    ahead = HG if k < 2 else HG - 1
                    if not (first and k == 0):
                        copy_ac(b - 1, (k - 1) % GB, it if k == 1 and not first else None)
                    if k == 2 and not first:
                        copy_xgT(it - 1)
                    if not (last and k >= GB - 2):
                        exps(b + 1, (k + 1) % GB, range(ahead))
                    if not (first and k == 0 or last and k > 0):
                        ctx_apply(it + (k + 3) // GB, (k + 3) % GB)
                    if k == 0 and not first:
                        copy_out(it - 1)
                    if k == 1 and not last:
                        copy_qk(it + 1)
                    copy_pT(b, (0, 1), first and k == 0)
                    if not (last and k >= GB - 2):
                        exps(b + 1, (k + 1) % GB, range(ahead, HG))
                    if k == 2 and not first:
                        local_qk(it - 1)
                    if not (last and k > 0):
                        copy_cT(b + 3, k + 1)
                    copy_pT(b, (2,))
                    if k == 3 and not first:
                        copy_plT(it - 1)
                    copy_pT(b, (3,))
                    if last and k == 1:
                        exps(b + 2, k + 2)
                    if k == 2 and not first:
                        local_exp(it - 1)

            act.wait_ge(biases_ready, 1)
            body(0, first=True)
            with act.Fori(1, G - 1) as it:
                body(it)
            body(G - 1, last=True)
            copy_ac(B - 1, GB - 1)
            copy_out(G - 1)

            def copy_fnT(p):
                act.wait_ge(ffn_xT_ready, p + 1)
                act.copy(fnT[:, PASS[p][1]], (pA, pC)[p][:, 0:len(PASS[p][0]) * P]).then_inc(ffn_xT_copied, 1)

            def activate(n):
                toks = PASS[0][1]
                if n >= 2:
                    act.wait_ge(hT_ready, n * 2 - 2)
                for i in range(2):
                    act.wait_ge(hidden_ready, n * 2 + i + 1)
                    act.activation(hs[n % 2][:, i, toks], (pS, pP)[i][0][:, toks], ACT.Gelu_apprx_sigmoid,
                                   bias=b1g[:, n, i:i + 1])
                    act.activation(hv[n % 2][:, i, toks], (pS, pP)[i][1][:, toks], ACT.Identity,
                                   bias=b1v[:, n, i:i + 1]).then_inc(activated, 1)

            def activate2(e):
                toks, n, odd = PASS[1][1], E + e, e % 2
                act.wait_ge(hT_ready, n * 2 - 2)
                act.wait_ge(hidden_ready, n * 2 + 2)
                for i in range(2):
                    bank = slice(i * P, (i + 1) * P)
                    act.activation(hs[odd][:, i, toks], (pS, pP)[odd][0][:, bank], ACT.Gelu_apprx_sigmoid,
                                   bias=b1g[:, e, i:i + 1])
                    act.activation(hv[odd][:, i, toks], (pS, pP)[odd][1][:, bank], ACT.Identity,
                                   bias=b1v[:, e, i:i + 1]).then_inc(activated, 1)

            def gate_exp(p):
                act.wait_ge(gate_diff_ready, p + 1)
                gs = slice(PASS[p][0][0], PASS[p][0][-1] + 1)
                act.activation(gp2[:, gs], gd[:, gs], ACT.Exp).then_inc(gate_exp_done, 1)

            copy_fnT(0)
            activate(0)
            activate(1)
            gate_exp(0)
            copy_xgT(G - 1)
            local_qk(G - 1)
            activate(2)
            activate(3)
            local_exp(G - 1)
            activate(4)
            copy_plT(G - 1)
            activate(5)
            activate(6)
            activate(7)
            copy_fnT(1)
            for e in range(E):
                if e == 1:
                    gate_exp(1)
                if e == 4:
                    act.wait_ge(weightsT_ready, 1)
                    act.copy(gwT[:, :], pM[0][0:E, :]).then_inc(weightsT_copied, 1)
                activate2(e)

        @block.tensor
        def _(pe):
            def head_products(L, R, banks, q, done):
                for a in range(2):
                    for e in range(2):
                        ins = pe.matmul(banks[q % 2][e][:, a * C:(a + 1) * C], L[64 * e:64 * e + 64, 2 * q + a, :],
                                        R[64 * e:64 * e + 64, 2 * q + a, :], start=True, stop=True)
                ins.then_inc(done, 1)

            pe.wait_ge(ld_wq, 16)
            pe.wait_ge(nk_placed, 1)
            for c in range(KC):
                ins = pe.matmul(pC[:, 0:P], WqT[:, c, :], NKblk[:, c * P:(c + 1) * P], start=(c == 0), stop=(c == KC - 1))
            ins.then_inc(u_ready, 1)
            pe.wait_ge(ld_wk, 16)
            for q in range(H // 4):
                if q >= 2:
                    pe.wait_ge(wA_copied, q - 1)
                head_products(WqT, WkT, (pP, pS), q, wA_ready)

            def value_products(q):
                if q == 0:
                    pe.wait_ge(ld_wvT, 16)
                    pe.wait_ge(ld_wo, 16)
                    pe.wait_ge(wA_copied, 3)
                if q >= 2:
                    pe.wait_ge(wB_copied, q - 1)
                head_products(WvT, Wo, (pP, pM), q, wB_ready)

            value_products(0)
            value_products(1)
            pe.wait_ge(wA_copied, H // 4)
            pe.wait_ge(x_normed, 1)
            pe.wait_ge(ld_con, 16)
            for g in range(G):
                ins = pe.transpose(pS[1][:, g * P:(g + 1) * P], rowtmp[:, g, :], ident)
            ins.then_inc(xT_ready, 1)
            pe.wait_ge(xT_copied, 1)
            pe.wait_ge(u_copied, 1)
            pe.matmul(pS[0][:, :], U[:, :], xnT[:, :], start=True, stop=True).then_inc(sn_ready, 1)

            def qk(g, first=False):
                for q in range(HG):
                    if not (first and q < 2):
                        pe.wait_ge(qk_copied, g * HG + q - 1)
                    for h in range(4):
                        ins = pe.matmul(pM[q % 2][:, h * P:(h + 1) * P], A[:, 4 * q + h, :],
                                        xnT[:, bass.ds(g * P, P)], start=True, stop=True)
                    ins.then_inc(qk_ready, 1)

            def ctx_T(b, k, first=False):
                pe.wait_ge(ctx_normed, b + 1)
                if not isinstance(b, int) or b >= GB:
                    pe.wait_ge(tile_normed, b + 1 - GB)
                if not first:
                    pe.wait_ge(cT_copied, b)
                for t in range(T):
                    ins = pe.transpose(pC[:, t * P:(t + 1) * P], NC[:, k, t, :], ident)
                ins.then_inc(cT_ready, 1)

            def scores(b, k, g, quartets=range(HG), first=False):
                if 0 in quartets:
                    pe.wait_ge(cT_copied, b + 1)
                    if k == 0:
                        pe.wait_ge(qk_copied, g * HG + HG)
                for q in quartets:
                    if not (first and q < 2):
                        pe.wait_ge(masked, b * HG + q - 1)
                    pe.matmul(pS[q % 2][:, :], QK[:, k, 4 * q:4 * q + 4, :].rearrange("p h i -> p (h i)"),
                              cnT[:, k % 2, :], start=True, stop=True).then_inc(scores_ready, 1)

            def probs_T(b, k, t, first=False):
                if t == 0:
                    pe.wait_ge(probs_normed, b * HG + HG)
                if not (first and t < 2):
                    pe.wait_ge(pt_copied, b * T + t - 1)
                for q in range(HG):
                    ins = pe.transpose(pP[t % 2][:, q * P:(q + 1) * P], SM[:, k, q, t * P:(t + 1) * P], ident)
                ins.then_inc(probsT_ready, 1)

            def pv(b, k, t, first=False):
                if t == 0 and not first:
                    pe.wait_ge(ac_copied, b)
                pe.wait_ge(pt_copied, b * T + t + 1)
                ins = pe.matmul(pA[:, :], NC[:, k, t, :], PT[:, t, :], start=(t == 0), stop=(t == T - 1))
                if t == T - 1:
                    ins.then_inc(pv_ready, 1)

            pe.wait_ge(ld_wv, 16)
            pe.wait_ge(ld_vec, 16)
            for c in range(KC):
                ins = pe.matmul(pA[:, c:c + 1], Wv[:, c * P:(c + 1) * P], VEC[:, V_LNCB:V_LNCB + 1], start=True, stop=True)
            ins.then_inc(vb_ready, 1)
            pe.wait_ge(sn_copied, 1)
            pe.wait_ge(wB_copied, 2)
            qk(0, True)
            ctx_T(0, 0, True)
            value_products(2)
            scores(0, 0, 0, first=True)
            ctx_T(1, 1)
            value_products(3)
            scores(1, 1, 0)
            pe.wait_ge(nv_placed, 1)
            for c in range(KC):
                ins = pe.matmul(pA[:, 0:C], NVblk[:, c * P:(c + 1) * P], Wo[:, c, :], start=(c == 0), stop=(c == KC - 1))
            ins.then_inc(nvw_ready, 1)
            ctx_T(2, 2)
            pe.wait_ge(nvw_copied, 1)
            pe.wait_ge(wB_copied, H // 4)

            def project(g, contexts):
                pe.wait_ge(cT_copied, contexts)
                pe.wait_ge(pnT_ready, g + 1)
                pe.wait_ge(ac_copied, g * GB + GB)
                for h in range(H):
                    pe.matmul(pC[:, 0:C], AC[:, h, :], Bm[:, h, :], start=(h == 0), stop=False)
                pe.matmul(pC[:, 0:C], PNT[:, :], NVW[:, :], start=False, stop=True).then_inc(out_ready, 1)

            def local_T(g, contexts):
                pe.wait_ge(cT_copied, contexts)
                pe.wait_ge(local_normed, g + 1)
                pe.transpose(pC[:, 0:P], xg[:, :], ident).then_inc(local_xT_ready, 1)

            def local_qkv(g):
                pe.wait_ge(local_xT_copied, g + 1)
                pe.matmul(pM[0][:, 0:P], Wqkv[:, 0:C], xgT[:, :], start=True, stop=True)
                ins = pe.matmul(pM[0][:, P:2 * P], Wqkv[:, C:2 * C], xgT[:, :], start=True, stop=True)
                ins.then_inc(local_keys_ready, 1)
                for b in range(GB):
                    ins = pe.matmul(pM[1][:, b * C:(b + 1) * C], XR[:, b, :, :].rearrange("p r i -> p (r i)"),
                                    Wqkv[:, 2 * C:3 * C], start=True, stop=True)
                ins.then_inc(local_values_ready, 1)

            def local_scores(g):
                pe.wait_ge(local_keys_placed, g + 1)
                pe.wait_ge(local_values_placed, g + 1)
                passed(pe, g)
                for half in range(2):
                    for b in range(GB):
                        for bank in range(2):
                            r = 2 * bank + half
                            ins = pe.matmul(pM[bank][N * b:N * b + N, half * LR * LJ:(half + 1) * LR * LJ],
                                            qT[32 * r:32 * r + 32, N * b:N * b + N],
                                            Kbd[32 * r:32 * r + 32, b, :, :].rearrange("p r j -> p (r j)"),
                                            start=True, stop=True)
                    ins.then_inc(local_scores_ready, 1)
                    if half == 0:
                        pe.wait_ge(local_scores_ready, g * 2 + 1)
                        passed(pe, g)

            def local_pT(g):
                pe.wait_ge(local_probs_ready, g + 1)
                for r in range(4):
                    ins = pe.transpose(pM[0][:, r * P:(r + 1) * P],
                                       PL[:, 4 * r:4 * r + 4, :].rearrange("p h j -> p (h j)"), ident)
                ins.then_inc(local_probsT_ready, 1)

            def local_pv(g):
                pe.wait_ge(local_probsT_copied, g + 1)
                passed(pe, g)
                for b in range(GB):
                    for r in range(4):
                        ins = pe.matmul(pM[1][32 * r:32 * r + 32, N * b:N * b + N], Vbd[:, b, 32 * r:32 * r + 32],
                                        PLT[:, r, N * b:N * b + N], start=True, stop=True)
                ins.then_inc(local_oT_ready, 1)

            def local_out(g):
                pe.wait_ge(local_oT_copied, g + 1)
                pe.matmul(pM[1][:, P:2 * P], oT[:, :], Wout[:, :], start=True, stop=True).then_inc(local_y_ready, 1)

            def body(it, first=False, last=False):
                for k in range(GB):
                    b = it * GB + k
                    if not (last and k >= GB - 2):
                        scores(b + 2, (k + 2) % GB, it + (k + 2) // GB, range(0, 2))
                    probs_T(b, k, 0, first and k == 0)
                    if not (last and k >= GB - 2):
                        scores(b + 2, (k + 2) % GB, it + (k + 2) // GB, range(2, HG))
                    if k == 0 and not first:
                        project(it - 1, b + 3)
                    if k == 1 and not last:
                        qk(it + 1)
                    if k == 2 and not first:
                        local_qkv(it - 1)
                    probs_T(b, k, 1, first and k == 0)
                    if not (last and k > 0):
                        if k == 0 and not first:
                            pe.wait_ge(out_copied, it)
                        if k == 2 and not first:
                            pe.wait_ge(local_xT_copied, it)
                        ctx_T(b + 3, (k + 3) % GB)
                    probs_T(b, k, 2)
                    pv(b, k, 0, first and k == 0)
                    if k == 3 and not first:
                        local_pT(it - 1)
                    probs_T(b, k, 3)
                    pv(b, k, 1)
                    if k == 2 and not first:
                        local_scores(it - 1)
                    if k == 3 and not first:
                        local_pv(it - 1)
                    pv(b, k, 2)
                    if k == 3 and not first:
                        local_out(it - 1)
                    pv(b, k, 3)
                    if k == 1 and not first:
                        local_T(it - 1, B if last else b + 4)

            pe.wait_ge(ld_loc, 64)
            body(0, first=True)
            with pe.Fori(1, G - 1) as it:
                body(it)
            body(G - 1, last=True)
            project(G - 1, B)

            def gate(p):
                groups, toks = PASS[p]
                bank = (pA, pC)[p]
                pe.wait_ge(ffn_normed, p + 1)
                for i, g in enumerate(groups):
                    ins = pe.transpose(bank[:, i * P:(i + 1) * P], fn[:, g, :], ident)
                ins.then_inc(ffn_xT_ready, 1)
                pe.wait_ge(ffn_xT_copied, p + 1)
                for i, g in enumerate(groups):
                    ins = pe.matmul(bank[:, 384 + i * E:384 + (i + 1) * E], fnT[:, g * P:(g + 1) * P], Gate[:, :],
                                    start=True, stop=True)
                ins.then_inc(gate_ready, 1)

            def hidden(n):
                pe.wait_ge(ld_e[n], 32)
                for i in range(2):
                    if n:
                        pe.wait_ge(activated, n * 2 + i - 1)
                    for v in range(2):
                        ins = pe.matmul((pS, pP)[i][v][:, PASS[0][1]], W1s[n][:, v, i, :], fnT[:, PASS[0][1]],
                                        start=True, stop=True)
                    ins.then_inc(hidden_ready, 1)

            def hidden2(n):
                pe.wait_ge(activated, max(n - 1, E) * 2)
                for i in range(2):
                    for v in range(2):
                        ins = pe.matmul((pS, pP)[n % 2][v][:, i * P:(i + 1) * P], W1s[n - E][:, v, i, :],
                                        fnT[:, PASS[1][1]], start=True, stop=True)
                ins.then_inc(hidden_ready, 2)

            def down(p, n):
                pe.wait_ge(hT_ready, n * 2 + 2)
                if n:
                    pe.wait_ge(expert_added, n - p * (n > E))
                if n == 0 or n == E + 1:
                    pe.wait_ge(gate_copied, p + 1)
                bank = pC if p and n % 2 else pA
                for g in PASS[p][0]:
                    for i in range(2):
                        ins = pe.matmul(bank[:, g * C:(g + 1) * C], hT[n % 2][:, i, g * P:(g + 1) * P],
                                        W2s[n % E][:, i, :], start=(i == 0), stop=(i == 1))
                ins.then_inc(down_ready, 1)

            pe.wait_ge(ac_copied, B)
            gate(0)
            hidden(0)
            hidden(1)
            hidden(2)
            pe.wait_ge(out_copied, G)
            local_T(G - 1, B)
            down(0, 0)
            local_qkv(G - 1)
            down(0, 1)
            hidden(3)
            down(0, 2)
            local_scores(G - 1)
            hidden(4)
            down(0, 3)
            local_pT(G - 1)
            hidden(5)
            local_pv(G - 1)
            down(0, 4)
            local_out(G - 1)
            hidden(6)
            down(0, 5)
            hidden(7)
            down(0, 6)
            gate(1)
            hidden2(E)
            down(0, E - 1)
            hidden2(E + 1)
            for e in range(1, E):
                if e < E - 1:
                    hidden2(E + e + 1)
                if e == 2:
                    pe.wait_ge(weights_ready, 2)
                    for g in range(G):
                        ins = pe.transpose(pM[0][0:E, g * P:(g + 1) * P], gw[:, g, :], ident)
                    ins.then_inc(weightsT_ready, 1)
                if e == 4:
                    pe.wait_ge(weightsT_copied, 1)
                    for g in range(G):
                        ins = pe.matmul(pM[1][:, g * C:(g + 1) * C], gwT[:, g * P:(g + 1) * P], B2[:, :],
                                        start=True, stop=True)
                    ins.then_inc(bias_sum_ready, 1)
                down(1, E + e - 1)
            down(1, 2 * E - 1)

        @block.vector
        def _(dve):
            ch = Chain(dve, dve_step)
            link = ch.link

            def norm_rows(dst, src, eps, n):
                passed(dve, ch.base)
                for g in range(n):
                    ins = dve.bn_stats(xstat[:, g, :], src(g))
                link(ins)
                passed(dve, ch.base)
                for g in range(n):
                    ins = dve.bn_aggr(xmv[:, g, :], xstat[:, g, :])
                link(ins)
                inv_sqrt(dve, link, (nt_v, nt_a), xrs[:, 0:n], xmv[:, 0:n, 1], eps, n, True)
                for g in range(n):
                    ins = dve.tensor_scalar(dst(g), src(g), xmv[:, g, 0:1], xrs[:, g:g + 1], ALU.subtract, ALU.mult)
                return ins

            def place(blk, src, done):
                for e in range(2):
                    for kp in range(2):
                        start = kp * 192 + 32 * e
                        ins = dve.tensor_copy(blk[64 * e:64 * e + 64, start:start + 3 * 257 + 1:257], src(e, kp))
                ins.then_inc(done, 1)

            dve.wait_ge(ld_vec, 16)
            dve.wait_ge(blk_zero, 3)
            place(NKblk, lambda e, kp: VEC[64 * e:64 * e + 64, V_NK:V_NK + 1].broadcast_to([64, 4]), nk_placed)
            dve.wait_ge(ld_x, 16)
            link(norm_rows(lambda g: rowtmp[:, g, :], lambda g: X[:, g, :], 1e-5, G))
            norm_rows(lambda g: rowtmp[:, g, :], lambda g: rowtmp[:, g, :], 1e-6, G).then_inc(x_normed, 1)

            def ctx_stats(g, k):
                passed(dve, g)
                for t in range(T):
                    src = CTX[:, GB * g + k, t, :] if isinstance(g, int) else col(CTX, g * GB + k)[:, t, :]
                    ins = dve.bn_stats(cstat[:, k * T + t, :], src)
                return ins

            def ctx_moments(g, k):
                ctx_stats(g, k)
                link(ctx_stats(g, k + 1))
                passed(dve, ch.base)
                for i in range(k * T, (k + 2) * T):
                    ins = dve.bn_aggr(cmv[:, i, :], cstat[:, i, :])
                return ins

            def first_norm(k):
                for b in (k, k + 1):
                    for t in range(T):
                        i = b * T + t
                        ins = dve.tensor_scalar(NC[:, b, t, :], CTX[:, b, t, :], cmv[:, i, 0:1], crs[:, i:i + 1],
                                                ALU.subtract, ALU.mult)
                    ins.then_inc(ctx_normed, 1)

            dve.wait_ge(ld_ctx[0], 16)
            link(ctx_moments(0, 0))
            inv_sqrt(dve, link, (nt_v, nt_a), crs[:, 0:2 * T], cmv[:, 0:2 * T, 1], 1e-6, 2 * T, True)
            first_norm(0)
            dve.wait_ge(sn_copied, 1)
            link(dve.transpose(SNR[:, :, :].rearrange("p b g -> p (b g)"), sn_pad[:, :]))
            dve.wait_ge(vb_ready, 1)
            link(dve.tensor_scalar(nvk[:, :], pA[:, 0:KC], -1.0, VEC[:, V_NV:V_NV + 1], ALU.mult, ALU.add))
            place(NVblk, lambda e, kp: nvk[64 * e:64 * e + 64, kp:KC:2], nv_placed)
            ctx_moments(0, 2).then_inc(moments_ready, 1)

            def ctx_apply_tile(g, k):
                n = k * T + T - 1
                if k % 2 == 0:
                    dve.wait_ge(inv_ready, g * 2 + k // 2)
                    passed(dve, g)
                dve.tensor_scalar(NC[:, k, T - 1, :], col(CTX, g * GB + k)[:, T - 1, :], cmv[:, n, 0:1],
                                  crs[:, n:n + 1], ALU.subtract, ALU.mult).then_inc(tile_normed, 1)

            def mask_max(b, k):
                dve.wait_ge(mask_ready, b + 1)
                for q in range(HG):
                    dve.wait_ge(scores_ready, b * HG + q + 1)
                    passed(dve, b)
                    ins = dve.tensor_tensor_reduce(SM[:, k, q, :], pS[q % 2][:, :], MB[:, k % 2, :], 1.0, -BIG,
                                                   ALU.add, ALU.max, mrow[:, k, q:q + 1])
                    ins.then_inc(masked, 1)
                dve.wait_ge(masked, b * HG + HG)
                null = col(SNR, b)[:, 0:HG]
                link(dve.tensor_tensor(mx4[:, :], mrow[:, k, :], null, ALU.max))
                link(dve.tensor_scalar(negm[:, k, :], mx4[:, :], -SCALE, None, ALU.mult))
                dve.scalar_tensor_tensor(snm[:, k, :], null, SCALE, negm[:, k, :], ALU.mult,
                                         ALU.add).then_inc(shift_ready, 1)

            def sums(b, k):
                dve.wait_ge(exp_done, (b + 1) * (HG + 1))
                link(dve.tensor_tensor(lsum[:, :], rsum[:, k, :], pn[:, k, :], ALU.add))
                link(dve.reciprocal(rinv[:, k, :], lsum[:, :]))
                for q in range(HG):
                    dve.tensor_scalar(SM[:, k, q, :], SM[:, k, q, :], rinv[:, k, q:q + 1], None,
                                      ALU.mult).then_inc(probs_normed, 1)
                link(dve.tensor_tensor(PNR[:, k, 0:HG], pn[:, k, :], rinv[:, k, :], ALU.mult))

            def local_norm1(g):
                dve.wait_ge(out_copied, g + 1)
                passed(dve, g)
                link(dve.bn_stats(ostat[:, :], OUT1[:, :]))
                passed(dve, g)
                link(dve.bn_aggr(omv[:, :], ostat[:, :]))
                inv_sqrt(dve, link, (nt_v, nt_a), ors[:, :], omv[:, 1:2], 1e-6, 1, True)
                dve.sem_inc(out_inv, 1)

            def local_norm2(g):
                xr = col(X, g)
                dve.wait_ge(x1_ready, g + 1)
                norm_rows(lambda _: xg[:, :], lambda _: xr, 1e-5, 1).then_inc(local_normed, 1)

            def local_v(g):
                dve.wait_ge(local_values_ready, g + 1)
                own = CON[:, K_V:K_V + C].unsqueeze(1).broadcast_to([P, GB, C])
                dve.tensor_tensor(Vbd[:, :, :], pM[1][:, :].rearrange("p (b c) -> p b c", b=GB), own,
                                  ALU.mult).then_inc(local_values_placed, 1)

            def local_max(g):
                dve.wait_ge(local_scores_ready, g * 2 + 2)
                views = [pM[i][:, 0:2 * LR * LJ].rearrange("p (h j) -> p h j", j=LJ) for i in range(2)]
                for i in range(2):
                    ins = dve.tensor_reduce(lmax[:, 8 * i:8 * i + 8], views[i], AX.X, ALU.max)
                link(ins)
                for i in range(2):
                    ins = dve.tensor_tensor(SL[:, 8 * i:8 * i + 8, :], views[i],
                                            lmax[:, 8 * i:8 * i + 8].unsqueeze(2).broadcast_to([P, 8, LJ]),
                                            ALU.subtract)
                ins.then_inc(local_shifted, 1)

            def local_probs(g):
                dve.wait_ge(local_exp_done, g + 1)
                link(dve.tensor_scalar(SL[:, :, N:LJ], SL[:, :, N:LJ], float(PADS), None, ALU.mult))
                link(dve.tensor_reduce(lden[:, :], SL[:, :, :], AX.X, ALU.add))
                link(dve.reciprocal(lrec[:, :], lden[:, :]))
                dve.tensor_tensor(PL[:, :, :], SL[:, :, 0:N], lrec[:, :].unsqueeze(2).broadcast_to([P, 16, N]),
                                  ALU.mult).then_inc(local_probs_ready, 1)

            def local_o(g):
                dve.wait_ge(local_oT_ready, g + 1)
                dve.tensor_scalar(oT[:, :], pM[1][:, 0:P], VEC[:, V_BV:V_BV + 1], None, ALU.add).then_inc(local_oT_copied, 1)

            def local_add(g):
                xr = col(X, g)
                dve.wait_ge(local_y_ready, g + 1)
                link(dve.tensor_tensor(xr, xr, pM[1][:, P:2 * P], ALU.add))
                link(dve.tensor_tensor(xr, xr, ROWS[:, 2, :], ALU.add))

            mask_max(0, 0)
            dve.wait_ge(inv_ready, 1)
            first_norm(2)
            mask_max(1, 1)
            sums(0, 0)
            for g in range(1, G):
                dve.wait_ge(ld_ctx[g], 16)
            dve.wait_ge(ld_rows, 16)
            b1 = VEC[:, V_B1:V_B1 + 4 * E].rearrange("p (e v i) -> p e v i", v=2, i=2)
            dve.tensor_copy(b1g[:, :, :], b1[:, :, 0, :])
            dve.tensor_scalar(b1v[:, :, :], b1[:, :, 1, :], 1.0, None, ALU.add)
            dve.tensor_scalar(qbias[:, :], VEC[:, V_BQ:V_BQ + 1], LD ** -0.5, None, ALU.mult)
            link(dve.tensor_scalar(kbias[:, :], CON[:, K_R:K_R + LR], VEC[:, V_BK:V_BK + 1], None, ALU.mult))
            for b in range(GB):
                ins = dve.tensor_copy(Kbd[:, b, :, N], kbias[:, :])
            ins.then_inc(biases_ready, 1)

            def body(it, first=False, last=False):
                for k in range(GB):
                    b = it * GB + k
                    tile = not (first and k == 0 or last and k > 0)
                    if tile:
                        dve.wait_ge(pv_ready, b)
                    if tile and k != 1:
                        ctx_apply_tile(it + (k + 3) // GB, (k + 3) % GB)
                    if not (last and k >= GB - 2):
                        mask_max(b + 2, (k + 2) % GB)
                    if tile and k == 1:
                        ctx_apply_tile(it + 1, 0)
                    if last and k == 2:
                        sums(b + 1, k + 1)
                    if k == 2 and not first:
                        local_v(it - 1)
                    if k == 3 and not first:
                        local_probs(it - 1)
                    if k == GB - 1:
                        if not first:
                            dve.wait_ge(out_ready, it)
                        dve.transpose(PNT[:, :], PNR[:, :, :].rearrange("p k g -> p (k g)")).then_inc(pnT_ready, 1)
                        dve.wait_ge(pnT_ready, it + 1)
                    if not last and k == 0:
                        ctx_moments(it + 1, 0).then_inc(moments_ready, 1)
                    if not (last and k >= GB - 2):
                        sums(b + 1, (k + 1) % GB)
                    if k == 1 and not first:
                        local_norm2(it - 1)
                    if not last and k == 1:
                        ctx_moments(it + 1, 2).then_inc(moments_ready, 1)
                    if k == 0 and not first:
                        local_norm1(it - 1)
                    if k == 2 and not first:
                        local_max(it - 1)
                    if k == 3 and not first:
                        local_o(it - 1)
                        local_add(it - 1)

            body(0, first=True)
            with dve.Fori(1, G - 1) as it:
                ch.loop(it - 1, BODY_STEPS)
                body(it)
            ch.end(G - 2)
            body(G - 1, last=True)

            def ffn_norm(groups):
                norm_rows(lambda i: fn[:, groups[i], :], lambda i: X[:, groups[i], :], 1e-5,
                          len(groups)).then_inc(ffn_normed, 1)

            def gate_best(p):
                gs = slice(PASS[p][0][0], PASS[p][0][-1] + 1)
                n = gs.stop - gs.start
                dve.wait_ge(gate_ready, p + 1)
                ins = dve.tensor_copy(gt[:, gs, :].rearrange("p g e -> p (g e)"), (pA, pC)[p][:, 384:384 + n * E])
                ins.then_inc(gate_copied, 1)
                dve.wait_ge(gate_copied, p + 1)

                def first_best(src, m, one_hot):
                    link(dve.tensor_reduce(m[:, gs], src[:, gs, :], AX.X, ALU.max))
                    link(dve.tensor_tensor(g_a[:, gs, :], src[:, gs, :], over_experts(m, gs), ALU.is_equal))
                    link(dve.tensor_tensor(g_a[:, gs, :], g_a[:, gs, :],
                                           CON[:, K_IOTA:K_IOTA + E].unsqueeze(1).broadcast_to([P, n, E]), ALU.mult))
                    link(dve.tensor_reduce(gi[:, gs], g_a[:, gs, :], AX.X, ALU.max))
                    link(dve.tensor_tensor(one_hot[:, gs, :], g_a[:, gs, :], over_experts(gi, gs), ALU.is_equal))

                first_best(gt, gm1, g_is1)
                link(dve.scalar_tensor_tensor(g_rest[:, gs, :], g_is1[:, gs, :], -BIG, gt[:, gs, :], ALU.mult, ALU.add))
                first_best(g_rest, gm2, g_is2)
                dve.tensor_tensor(gd[:, gs], gm2[:, gs], gm1[:, gs], ALU.subtract).then_inc(gate_diff_ready, 1)

            def over_experts(t, gs):
                return t[:, gs].unsqueeze(2).broadcast_to([P, gs.stop - gs.start, E])

            def gate_weights(p):
                gs = slice(PASS[p][0][0], PASS[p][0][-1] + 1)
                dve.wait_ge(gate_exp_done, p + 1)
                link(dve.tensor_scalar(gp1[:, gs], gp2[:, gs], 1.0, None, ALU.add))
                link(dve.reciprocal(gp1[:, gs], gp1[:, gs]))
                link(dve.tensor_tensor(gp2[:, gs], gp2[:, gs], gp1[:, gs], ALU.mult))
                link(dve.tensor_tensor(g_is1[:, gs, :], g_is1[:, gs, :], over_experts(gp1, gs), ALU.mult))
                link(dve.tensor_tensor(g_is2[:, gs, :], g_is2[:, gs, :], over_experts(gp2, gs), ALU.mult))
                dve.tensor_tensor(gw[:, gs, :], g_is1[:, gs, :], g_is2[:, gs, :], ALU.add).then_inc(weights_ready, 1)
                dve.wait_ge(weights_ready, p + 1)

            def swiglu(n):
                toks = PASS[0][1]
                for i in range(2):
                    dve.wait_ge(activated, n * 2 + i + 1)
                    dve.tensor_scalar(hv[n % 2][:, i, toks], hv[n % 2][:, i, toks], 1 - LIMIT, 1 + LIMIT, ALU.max,
                                      ALU.min).then_inc(clipped, 1)
                for i in range(2):
                    dve.wait_ge(clipped, n * 2 + i + 1)
                    if i == 0 and n >= 2:
                        dve.wait_ge(down_ready, n - 1)
                    dve.scalar_tensor_tensor(hT[n % 2][:, i, toks], hs[n % 2][:, i, toks], TOP, hv[n % 2][:, i, toks],
                                             ALU.min, ALU.mult).then_inc(hT_ready, 1)

            def swiglu2(n, odd):
                toks = PASS[1][1]
                dve.wait_ge(activated, n * 2 + 2)
                dve.tensor_scalar(hv[odd][:, :, toks], hv[odd][:, :, toks], 1 - LIMIT, 1 + LIMIT, ALU.max,
                                  ALU.min).then_inc(clipped, 2)
                dve.wait_ge(clipped, n * 2 + 2)
                dve.wait_ge(down_ready, n - 1)
                dve.scalar_tensor_tensor(hT[odd][:, :, toks], hs[odd][:, :, toks], TOP, hv[odd][:, :, toks],
                                         ALU.min, ALU.mult).then_inc(hT_ready, 2)

            def add_expert(p, n, e, bank=pA):
                dve.wait_ge(down_ready, n + 1)
                if not (isinstance(n, int) and n == 0):
                    dve.wait_ge(expert_added, n)
                for g in PASS[p][0]:
                    ins = dve.scalar_tensor_tensor(X[:, g, :], bank[:, g * C:(g + 1) * C],
                                                   col(gw.rearrange("p g e -> p e g"), e)[:, g:g + 1], X[:, g, :],
                                                   ALU.mult, ALU.add)
                ins.then_inc(expert_added, 1)

            ffn_norm(PASS[0][0])
            local_norm1(G - 1)
            gate_best(0)
            local_norm2(G - 1)
            swiglu(0)
            gate_weights(0)
            swiglu(1)
            add_expert(0, 0, 0)
            local_v(G - 1)
            swiglu(2)
            add_expert(0, 1, 1)
            swiglu(3)
            add_expert(0, 2, 2)
            local_max(G - 1)
            local_probs(G - 1)
            swiglu(4)
            add_expert(0, 3, 3)
            local_o(G - 1)
            swiglu(5)
            add_expert(0, 4, 4)
            local_add(G - 1)
            ffn_norm(PASS[1][0])
            swiglu(6)
            add_expert(0, 5, 5)
            swiglu(7)
            add_expert(0, 6, 6)
            gate_best(1)
            add_expert(0, 7, 7)
            swiglu2(E, 0)
            gate_weights(1)
            with dve.Fori(0, E // 2 - 1) as it:
                for j in range(2):
                    e = it * 2 + 1 + j
                    swiglu2(e + E, 1 - j)
                    add_expert(1, e + E - 1, e - 1, (pA, pC)[j])
            swiglu2(2 * E - 1, 1)
            dve.wait_ge(bias_sum_ready, 1)
            dve.wait_ge(expert_added, E)
            n = (G - 1) * P
            most = X[:, 0:G - 1, :].rearrange("p g c -> p (g c)")
            dve.tensor_tensor(most, most, pM[1][:, 0:n], ALU.add).then_inc(out_done, 1)
            add_expert(1, 2 * E - 2, E - 2, pA)
            dve.wait_ge(expert_added, 2 * E - 1)
            link(dve.tensor_tensor(X[:, G - 1, :], X[:, G - 1, :], pM[1][:, n:G * P], ALU.add))
            dve.wait_ge(down_ready, 2 * E)
            dve.scalar_tensor_tensor(X[:, G - 1, :], pC[:, n:G * P], gw[:, G - 1, E - 1:E], X[:, G - 1, :], ALU.mult,
                                     ALU.add).then_inc(out_done, 1)


def kernel(**inputs):
    import numpy as np
    import concourse.bacc as bacc
    from concourse.bass_utils import run_bass_kernel_spmd as run

    a = {n: np.asarray(v) for n, v in inputs.items()}
    wq, wkv, wo = a["L0_xattn_Wq"], a["L0_xattn_Wkv"], a["L0_xattn_Wo"]
    nk, nv = a["L0_xattn_null_kv"]
    bqkv = a["L0_attn_b_qkv"].reshape(3, C)
    b1 = a["L0_ffn_dense_1_b"].reshape(E, 2, P, 2).transpose(2, 0, 3, 1).reshape(P, 4 * E)
    vec = np.concatenate([np.stack([a["L0_xattn_ln1_s"], a["L0_xattn_ln1_b"], a["L0_xattn_lnc_s"], a["L0_xattn_lnc_b"],
                                    bqkv[0], bqkv[1], bqkv[2], np.concatenate([nk, nk]), np.concatenate([nv, nv])],
                                   axis=1), b1], axis=1)
    rows = np.stack([a["L0_xattn_lno_s"], a["L0_xattn_lno_b"], a["L0_attn_b_out"]])[None]
    ch = np.arange(P)
    const = np.zeros((P, K_COLS), np.float32)
    const[:, K_ID:K_ID + P] = np.eye(P)
    const[:, K_R:K_R + LR] = (ch[:, None] // LD) % LR == np.arange(LR)[None]
    const[:, K_V:K_V + C] = ch[:, None] // N == (ch[None] // LD) % LR
    const[:, K_IOTA:K_IOTA + E] = E - np.arange(E)
    w1 = a["L0_ffn_dense_1_w"].reshape(E, 2, P, 2, C).transpose(0, 4, 3, 1, 2)
    w2 = a["L0_ffn_dense_2_w"].reshape(E, C, 2, P).transpose(0, 3, 2, 1)
    mask = a["mask_BxS2_bf1"].view(np.uint8).reshape(B, P, T).transpose(0, 2, 1).reshape(1, B * M)
    arrays = {
        "x": a["x"].reshape(B * N, C), "ctx_in": a["ctx_1024"].reshape(B * M, C), "mask": mask, "vec": vec,
        "rows": rows, "const": const, "wqT": wq.T, "wkT": wkv[:, :H * D].T, "wvT": wkv[:, H * D:].T,
        "wv": wkv[:, H * D:], "wo": wo, "wqkv": a["L0_attn_w_qkv"], "wout": a["L0_attn_w_out"],
        "gate": a["L0_ffn_gate_w"], "w1": w1, "w2": w2, "b2": a["L0_ffn_dense_2_b"],
    }
    arrays = {f"{n}_dram": np.ascontiguousarray(v) for n, v in arrays.items()}
    nc = bacc.Bacc("TRN2", target_bir_lowering=False, num_devices=1)
    aps = [nc.dram_tensor(n, v.shape, mybir.dt.from_np(v.dtype), kind="ExternalInput").ap() for n, v in arrays.items()]
    out = nc.dram_tensor("out_dram", (B * N, C), F32, kind="ExternalOutput").ap()
    perceiver(nc, *aps, out)
    result = run(nc, [arrays], core_ids=[0])
    return result.results[0]["out_dram"].reshape(B, N, C)
```
